# Optimizing a Trainium2 kernel written in Bass

```python
import numpy as np
import jax
import jax.numpy as jnp

def _softmax(x, axis=-1):
    return jax.nn.softmax(x, axis=axis)

def _gelu(x):
    return jax.nn.gelu(x, approximate=True)

def _silu(x):
    return jax.nn.silu(x)

def _sigmoid(x):
    return jax.nn.sigmoid(x)

def _layernorm(x, axis=-1, eps=1e-05):
    m = jnp.mean(x, axis=axis, keepdims=True)
    v = jnp.var(x, axis=axis, keepdims=True)
    return (x - m) / jnp.sqrt(v + eps)

def _scatter_add(tgt, idx, src, axis=0):
    return tgt.at[idx].add(src)

def _segment_sum(src, seg, n):
    return jax.ops.segment_sum(src, seg, n)
kernel_name = 'mk_macaron_d1_jaxref_r4_f77b80'

def setup_inputs(seed: int=0):
    np.random.seed(seed)
    _w = jnp.asarray

    def _L0_attn_setup():
        import jax, jax.numpy as jnp
        import numpy as np
        B, S, D = (4, 512, 256)
        KD, VD = (256, 256)
        key = jax.random.key(seed)
        ks = jax.random.split(key, 9)
        sc_in = 1.0 / np.sqrt(D)
        sc_v = 1.0 / np.sqrt(VD)
        return {'x': jax.random.normal(ks[0], (B, S, D), dtype=jnp.float32), 'Wq': jax.random.normal(ks[1], (KD, D), dtype=jnp.float32) * sc_in, 'bq': jax.random.normal(ks[2], (KD,), dtype=jnp.float32) * 0.01, 'Wk': jax.random.normal(ks[3], (KD, D), dtype=jnp.float32) * sc_in, 'bk': jax.random.normal(ks[4], (KD,), dtype=jnp.float32) * 0.01, 'Wv': jax.random.normal(ks[5], (VD, D), dtype=jnp.float32) * sc_in, 'bv': jax.random.normal(ks[6], (VD,), dtype=jnp.float32) * 0.01, 'Wo': jax.random.normal(ks[7], (D, VD), dtype=jnp.float32) * sc_v, 'bo': jax.random.normal(ks[8], (D,), dtype=jnp.float32) * 0.01}
    _L0_attn_in = _L0_attn_setup()

    def _L0_ffn_setup():
        import jax, jax.numpy as jnp
        import numpy as np
        B, S, D = (4, 512, 256)
        P = 9
        DM = D // 4
        EPS = 1e-05

        def _mix(x, mix_kernel):
            xp = jnp.pad(x, ((0, 0), (1, 1), (0, 0)))
            return mix_kernel[0] * xp[:, :-2] + mix_kernel[1] * xp[:, 1:-1] + mix_kernel[2] * xp[:, 2:]

        def _layernorm(h, gamma, beta):
            mu = jnp.mean(h, axis=-1, keepdims=True)
            var = jnp.var(h, axis=-1, keepdims=True)
            return (h - mu) * jax.lax.rsqrt(var + EPS) * gamma + beta
        key = jax.random.key(seed)
        ks = jax.random.split(key, 12)
        sc_in = 1.0 / np.sqrt(D)
        sc_mid = 1.0 / np.sqrt(DM)
        return {'x': jax.random.normal(ks[0], (B, S, D), dtype=jnp.float32), 'mix_kernel': jax.random.normal(ks[1], (3, D), dtype=jnp.float32) * 0.5, 'W1': jax.random.normal(ks[2], (P, D, DM), dtype=jnp.float32) * sc_in, 'b1': jnp.zeros((P, DM), dtype=jnp.float32), 'W2': jax.random.normal(ks[3], (P, DM, D), dtype=jnp.float32) * sc_mid, 'b2': jnp.zeros((P, D), dtype=jnp.float32), 'Wo1': jax.random.normal(ks[4], (D, DM), dtype=jnp.float32) * sc_in, 'bo1': jnp.zeros((DM,), dtype=jnp.float32), 'Wo2': jax.random.normal(ks[5], (DM, P), dtype=jnp.float32) * sc_mid, 'bo2': jnp.zeros((P,), dtype=jnp.float32), 'gamma': jnp.ones((D,), dtype=jnp.float32), 'beta': jnp.zeros((D,), dtype=jnp.float32)}
    _L0_ffn_in = _L0_ffn_setup()
    _d = {'L0_attn_x': _L0_attn_in['x'], 'L0_attn_Wq': _L0_attn_in['Wq'], 'L0_attn_bq': _L0_attn_in['bq'], 'L0_attn_Wk': _L0_attn_in['Wk'], 'L0_attn_bk': _L0_attn_in['bk'], 'L0_attn_Wv': _L0_attn_in['Wv'], 'L0_attn_bv': _L0_attn_in['bv'], 'L0_attn_Wo': _L0_attn_in['Wo'], 'L0_attn_bo': _L0_attn_in['bo'], 'L0_ffn_mix_kernel': _L0_ffn_in['mix_kernel'], 'L0_ffn_W1': _L0_ffn_in['W1'], 'L0_ffn_b1': _L0_ffn_in['b1'], 'L0_ffn_W2': _L0_ffn_in['W2'], 'L0_ffn_b2': _L0_ffn_in['b2'], 'L0_ffn_Wo1': _L0_ffn_in['Wo1'], 'L0_ffn_bo1': _L0_ffn_in['bo1'], 'L0_ffn_Wo2': _L0_ffn_in['Wo2'], 'L0_ffn_bo2': _L0_ffn_in['bo2'], 'L0_ffn_gamma': _L0_ffn_in['gamma'], 'L0_ffn_beta': _L0_ffn_in['beta']}
    _x0 = _d['L0_attn_x']
    _d['L0_attn_x'] = jax.random.normal(jax.random.fold_in(jax.random.key(seed), 1), (2, 4096, 256), dtype=_x0.dtype)
    del _x0
    return _d

def reference(L0_attn_x, L0_attn_Wq, L0_attn_bq, L0_attn_Wk, L0_attn_bk, L0_attn_Wv, L0_attn_bv, L0_attn_Wo, L0_attn_bo, L0_ffn_mix_kernel, L0_ffn_W1, L0_ffn_b1, L0_ffn_W2, L0_ffn_b2, L0_ffn_Wo1, L0_ffn_bo1, L0_ffn_Wo2, L0_ffn_bo2, L0_ffn_gamma, L0_ffn_beta):

    def _L0_attn_ref(x, Wq, bq, Wk, bk, Wv, bv, Wo, bo):
        import jax, jax.numpy as jnp
        import numpy as np
        B, S, D = (4, 512, 256)
        KD, VD = (256, 256)
        q = jnp.einsum('bsd,kd->bsk', x, Wq) + bq
        k = jnp.einsum('bsd,kd->bsk', x, Wk) + bk
        v = jnp.einsum('bsd,vd->bsv', x, Wv) + bv
        scores = jnp.einsum('bqk,bsk->bqs', q, k) / jnp.sqrt(jnp.float32(KD))
        sign_mask = jnp.sign(scores)
        sign_mask = sign_mask + (sign_mask == 0).astype(jnp.float32)
        seq = scores.shape[-1]
        causal = jnp.tril(jnp.ones((seq, seq), dtype=bool))
        masked = jnp.where(causal, scores * sign_mask, -jnp.inf)
        weights = jax.nn.softmax(masked, axis=2)
        out = jnp.einsum('bqs,bsv->bqv', weights, v)
        return jnp.einsum('bqv,dv->bqd', out, Wo) + bo

    def _L0_ffn_ref(x, mix_kernel, W1, b1, W2, b2, Wo1, bo1, Wo2, bo2, gamma, beta):
        import jax, jax.numpy as jnp
        import numpy as np
        B, S, D = (4, 512, 256)
        P = 9
        DM = D // 4
        EPS = 1e-05

        def _mix(x, mix_kernel):
            xp = jnp.pad(x, ((0, 0), (1, 1), (0, 0)))
            return mix_kernel[0] * xp[:, :-2] + mix_kernel[1] * xp[:, 1:-1] + mix_kernel[2] * xp[:, 2:]

        def _layernorm(h, gamma, beta):
            mu = jnp.mean(h, axis=-1, keepdims=True)
            var = jnp.var(h, axis=-1, keepdims=True)
            return (h - mu) * jax.lax.rsqrt(var + EPS) * gamma + beta
        x_mixed = _mix(x, mix_kernel)
        h = jnp.einsum('bsd,pdm->bspm', x_mixed, W1) + b1
        stacked_paths = jnp.einsum('bspm,pmd->bspd', h, W2) + b2
        scores = jnp.tanh(x_mixed @ Wo1 + bo1) @ Wo2 + bo2
        idx = jnp.argmax(scores, axis=-1)
        weights = jax.nn.one_hot(idx, P, dtype=stacked_paths.dtype)
        collapsed = jnp.einsum('bspd,bsp->bsd', stacked_paths, weights)
        return _layernorm(x + collapsed, gamma, beta)
    x = L0_attn_x
    x = x + 0.5 * _L0_ffn_ref(_layernorm(x, axis=-1), L0_ffn_mix_kernel, L0_ffn_W1, L0_ffn_b1, L0_ffn_W2, L0_ffn_b2, L0_ffn_Wo1, L0_ffn_bo1, L0_ffn_Wo2, L0_ffn_bo2, L0_ffn_gamma, L0_ffn_beta)
    x = x + _L0_attn_ref(_layernorm(x, axis=-1), L0_attn_Wq, L0_attn_bq, L0_attn_Wk, L0_attn_bk, L0_attn_Wv, L0_attn_bv, L0_attn_Wo, L0_attn_bo)
    x = x + 0.5 * _L0_ffn_ref(_layernorm(x, axis=-1), L0_ffn_mix_kernel, L0_ffn_W1, L0_ffn_b1, L0_ffn_W2, L0_ffn_b2, L0_ffn_Wo1, L0_ffn_bo1, L0_ffn_Wo2, L0_ffn_bo2, L0_ffn_gamma, L0_ffn_beta)
    return x

_drawn_inputs = setup_inputs


def setup_inputs(seed=0):
    import zlib

    import numpy as np

    out = dict(_drawn_inputs(seed))
    spreads = {'L0_ffn_b1': (0.0, 0.1),
     'L0_ffn_b2': (0.0, 0.1),
     'L0_ffn_bo1': (0.0, 0.1),
     'L0_ffn_bo2': (0.0, 0.1),
     'L0_ffn_gamma': (1.0, 0.2),
     'L0_ffn_beta': (0.0, 0.1)}
    factors = {'L0_attn_bq': 47.499, 'L0_attn_bk': 30.766, 'L0_attn_bv': 2.688, 'L0_attn_bo': 3.399}
    for name, (base, spread) in spreads.items():
        noise = np.random.default_rng([zlib.crc32(name.encode()), seed]).standard_normal(out[name].shape)
        drawn = base * np.exp(spread * noise) if base else spread * noise
        out[name] = jnp.asarray(drawn.astype(out[name].dtype))
    for name, factor in factors.items():
        out[name] = (out[name] * factor).astype(out[name].dtype)
    return out
```

```python
import concourse.bass as bass
from concourse import mybir
from contextlib import ExitStack

F32 = mybir.dt.float32
F16 = mybir.dt.float16
ALU = mybir.AluOpType
ACT = mybir.ActivationFunctionType
AX = mybir.AxisListType

P = 128
B, S, D = 2, 4096, 256
NP, DM = 9, 64
DC = D // P
TT = 512
SUB = TT // P
NT = S // TT
HC = (DM + NP * DM) // P
EPS = 1e-5

XS = 64.0
WS = 64.0
QS = 32.0
BETA = 1.0 / 16
P_LOG = 8.317766166719343
MASKED = -1e30

RING = 10


def macaron(nc, x, Wq, bq, Wk, bk, Wv, bv, Wo, bo, mix, W1, b1, W2, b2, Wo1, bo1, Wo2, bo2,
            gamma, beta, out):
    x1 = nc.dram_tensor("x1_scratch", (B, S, D), F32, kind="Internal").ap()
    x2 = nc.dram_tensor("x2_scratch", (B, S, D), F32, kind="Internal").ap()

    def tiles(a):
        return a.rearrange("b (t u p) d -> (b t) p u d", u=SUB, p=P)

    x_t, x1_t, x2_t, out_t = tiles(x), tiles(x1), tiles(x2), tiles(out)

    ctx = ExitStack()
    with ctx:
        def sb(name, shape, dt=F32):
            return ctx.enter_context(nc.sbuf_tensor(name, shape, dt))

        def sem(name):
            return ctx.enter_context(nc.semaphore(name))

        R1 = sb("R1", [P, RING * SUB * TT])
        R2 = sb("R2", [P, 16384])
        R3 = sb("R3", [P, NT * SUB * D])

        class Region:

            def __init__(self, tensor):
                self.tensor, self.at = tensor, 0

            def take(self, n, dt=F32):
                words = n if dt == F32 else n // 2
                part = self.tensor[:, self.at:self.at + words]
                self.at += words
                assert self.at <= self.tensor.shape[1]
                return part if dt == F32 else part.bitcast(dt)

        f1, f2 = Region(R1), Region(R2)
        X = f1.take(NT * SUB * D)
        NTC = S + 2
        nT = f1.take(DC * NTC)
        Ns = f1.take(2 * SUB * D)
        N = R3[:, :]
        hb = f2.take(HC * TT)
        hm = f2.take(2 * TT)
        hhi = f2.take(HC * TT, F16)
        hlo = f2.take(HC * TT, F16)
        xa = f2.take(DC * TT)
        xm = f2.take(DC * TT)
        xhi = f2.take(DC * TT, F16)
        xlo = f2.take(DC * TT, F16)
        y = f2.take(SUB * D)
        z = f2.take(SUB * D)
        xb = f2.take(SUB * D)
        a1, a2, a3 = Region(R1), Region(R2), Region(R3)
        ring = a1.take(RING * SUB * TT)
        KT_hi = a2.take(DC * S, F16)
        KT_lo = a2.take(DC * S, F16)
        KV_hi = a2.take(S // P * D, F16)
        KV_lo = a2.take(S // P * D, F16)
        q_hi = a3.take(2 * DC * TT, F16)
        q_lo = a3.take(2 * DC * TT, F16)
        pf = a3.take(2 * TT)
        p_hi = a3.take(SUB * TT, F16)
        p_lo = a3.take(SUB * TT, F16)
        U = a3.take(DC * TT)
        xr = a3.take(SUB * D)

        run_max = sb("run_max", [P, TT])
        max_row = sb("max_row", [P, TT])
        max_col = sb("max_col", [P, SUB])
        rden = sb("rden", [P, SUB])
        w1_hi = sb("w1_hi", [P, DC, HC * P], F16)
        w1_lo = sb("w1_lo", [P, DC, HC * P], F16)
        w2_hi = sb("w2_hi", [P, HC, D], F16)
        w2_lo = sb("w2_lo", [P, HC, D], F16)
        wqk_hi = sb("wqk_hi", [P, DC, D], F16)
        wqk_lo = sb("wqk_lo", [P, DC, D], F16)
        wvo = sb("wvo", [P, DC, D + 8])
        wo2 = sb("wo2", [DM + 1, NP])
        b1c = sb("b1c", [P, HC])
        bo1c = sb("bo1c", [DM, 1])
        kmix = sb("kmix", [P, DC, 3])
        gamma_b = sb("gamma_b", [P, D])
        beta_b = sb("beta_b", [P, D])
        bo_b = sb("bo_b", [P, D])
        ident = sb("ident", [P, P])
        ident16 = sb("ident16", [P, P], F16)
        tri = sb("tri", [P, P])
        expand = sb("expand", [NP, HC, P], F16)
        prio = sb("prio", [P, SUB, NP])
        half = sb("half", [P, SUB])
        th = sb("th", [DM + 1, TT])
        oh = sb("oh", [P, SUB, NP], F16)
        oh_t = sb("oh_t", [NP, TT], F16)
        r_max = sb("r_max", [P, SUB])
        r_eq = sb("r_eq", [P, SUB, NP])
        r_pr = sb("r_pr", [P, SUB, NP])
        r_top = sb("r_top", [P, SUB])
        st = sb("st", [P, 2, SUB, 6])
        mv = sb("mv", [P, 2, SUB, 2])
        rstd = sb("rstd", [P, 2, SUB])
        veps = sb("veps", [P, 2, SUB])
        s1 = Region(R1)
        wqkv_s = s1.take(3 * DC * D)
        wo_s = s1.take(DC * D)
        wo_t = s1.take(DC * D)
        w1_s = s1.take(DC * HC * P)
        w2_s = s1.take(HC * D)
        bqkv_s = s1.take(8)
        off_s = s1.take(8)
        b1_s = s1.take(8)

        PS = ctx.enter_context(nc.psum_tensor("PS", [P, 8, TT], F32))
        ps_h, ps_m, ps_o, ps_r = PS[:, 0:2, :], PS[:, 2:4, :], PS[:, 4:6, :], PS[:, 6, :]
        ps_oh = PS[:, 7, :].bitcast(F16)
        ps_s, ps_u, ps_x = PS[:, 0:4, :], PS[:, 4:6, :], PS[:, 6:8, :]

        ps_route = ps_r[:, 0:SUB * 16].rearrange("p (u e) -> p u e", u=SUB)[:, :, 0:NP]

        waited = sem("waited")
        phase_done, weights_in, w2_cleared = sem("phase_done"), sem("weights_in"), sem("w2_cleared")
        pool_const, fold_step, folded, woT_psum = sem("pool_const"), sem("fold_step"), sem("folded"), sem("woT_psum")
        woT_done, wqk_psum, wvo_psum = sem("woT_done"), sem("wqk_psum"), sem("wvo_psum")
        x_in = [sem(f"x_in{i}") for i in range(4)]
        n_stat, n_var, n_eps, n_rstd, n_done, n_kept = (sem("n_" + s) for s in ("stat", "var", "eps", "rstd", "done", "kept"))
        r_stat, r_var, r_eps, r_rstd, r_mid = (sem("r_" + s) for s in ("stat", "var", "eps", "rstd", "mid"))
        a_stat, a_var, a_eps, a_rstd, a_done = (sem("a_" + s) for s in ("stat", "var", "eps", "rstd", "done"))
        nT_psum, nT_done, edges_set = sem("nT_psum"), sem("nT_done"), sem("edges_set")
        xa_done, mix_part, mix_done = sem("xa_done"), sem("mix_part"), sem("mix_done")
        xhi_done, xlo_done = sem("xhi_done"), sem("xlo_done")
        h_psum, hb_done, tanh_done = sem("h_psum"), sem("hb_done"), sem("tanh_done")
        route_psum, route_step, oh_done = sem("route_psum"), sem("route_step"), sem("oh_done")
        ohT_psum, ohT_done, mask_psum = sem("ohT_psum"), sem("ohT_done"), sem("mask_psum")
        hm_done, hhi_done, hlo_done = sem("hm_done"), sem("hhi_done"), sem("hlo_done")
        o_psum, y_done, xb_done, x1_done, stored = (sem("o_psum"), sem("y_done"), sem("xb_done"), sem("x1_done"),
                                                    sem("stored"))
        a_hi, a_lo, aT_psum, aT_hi, aT_lo = sem("a_hi"), sem("a_lo"), sem("aT_psum"), sem("aT_hi"), sem("aT_lo")
        q_psum, q_hi_done, spare_free = sem("q_psum"), sem("q_hi_done"), [sem("spare_free0"), sem("spare_free1")]
        s_psum, abs_done, tri_done, max_done = sem("s_psum"), sem("abs_done"), sem("tri_done"), sem("max_done")
        maxT_psum, maxrow_psum = sem("maxT_psum"), sem("maxrow_psum")
        sub_done, exp_done, phi_done, plo_done = sem("sub_done"), sem("exp_done"), sem("phi_done"), sem("plo_done")
        pv_done, u_done, out_psum, rden_done = sem("pv_done"), sem("u_done"), sem("out_psum"), sem("rden_done")
        xr_in, xr_bo, x2_done, x2_stored = sem("xr_in"), sem("xr_bo"), sem("x2_done"), sem("x2_stored")

        block = ctx.enter_context(nc.Block())
        LOADS = 23
        POOL_CONSTS = NP + 9

        def wait_apart(eng, semaphore, value):
            eng.wait_ge(semaphore, value)
            eng.sem_inc(waited, 1)

        def barrier(eng, k):
            eng.drain().then_inc(phase_done, 1)
            wait_apart(eng, phase_done, 5 * k)

        def after_ffn(ph, b):
            return 2 + 3 * b if ph == 0 else 2 + 3 * B + b

        def seq(ph, b):
            return (ph * B + b) * NT

        BLOCKS = SUB * NT * (NT + 1) // 2

        def within(eng, value, largest):
            if isinstance(value, int):
                return value
            return eng.snap(nc.s_assert_within(value, 0, largest, skip_runtime_bounds_check_because="loop bounds"))

        def blocks(eng, b, j, m):
            return within(eng, b * BLOCKS + 2 * (j * (j + 1)) + SUB * m, B * BLOCKS)

        def ring_at(eng, j, m):
            odd = j & 1
            at = (odd * (RING - 1) + m - 2 * (odd * m)) * (SUB * TT)
            return within(eng, at, (RING - 1) * SUB * TT)

        def keys_at(eng, j, n):
            return within(eng, n * -1 + j, NT - 1)

        def spare(j):
            return 2 * NT - 1 if isinstance(j, int) and j == NT - 1 else 2 + 2 * j
        SPARE = 2 * NT

        def has_q(j):
            return not isinstance(j, int) or j + 2 < NT

        def has_o(j):
            return not isinstance(j, int) or j >= 1

        def cols(a, at, n):
            return a[:, bass.ds(at, n)]

        def rows4(a):
            return a.rearrange("p (u d) -> p u d", u=SUB)

        def dram_tile(a, i):
            return a[bass.ds(i, 1)].rearrange("a p u d -> p (a u) d")

        def over_steps(eng, first, middle, last):
            first(0)
            with eng.Fori(1, NT - 2) as j:
                middle(j)
            last(NT - 2)
            last(NT - 1)

        def over_tiles(eng, tile):
            tile(0, True, False)
            with eng.Fori(1, NT - 1) as t:
                tile(t, False, False)
            tile(NT - 1, False, True)

        @block.sync
        def _(sp):
            def load(dst, src, columns=False):
                sp.dma_start(dst, src, allow_slow_non_contiguous=columns).then_inc(weights_in, 16)

            for i, w in enumerate((Wq, Wk, Wv)):
                load(wqkv_s[:, i * DC * D:(i + 1) * DC * D].rearrange("p (c d) -> p c d", c=DC),
                     w.rearrange("(c p) d -> p c d", p=P))
            for i, bias in enumerate((bq, bk, bv)):
                load(bqkv_s[:, DC * i:DC * i + DC], bias.rearrange("(c p) -> p c", p=P), columns=True)
            load(wo_s.rearrange("p (c d) -> p c d", c=DC), Wo.rearrange("(c p) d -> p c d", p=P))
            w1_v = w1_s.rearrange("p (c q m) -> p c q m", c=DC, m=DM)
            load(w1_v[:, :, 0, :], Wo1.rearrange("(c p) m -> p c m", p=P))
            for c in range(DC):
                load(w1_v[:, c, 1:, :], W1[:, c * P:(c + 1) * P, :].rearrange("e p m -> p e m"))
            b1_f = b1.rearrange("e m -> (e m)")
            load(b1_s[DM:P, 0:1], b1_f[0:DM].rearrange("(p a) -> p a", a=1))
            load(b1_s[:, 1:HC], b1_f[DM:].rearrange("(c p) -> p c", p=P), columns=True)
            load(bo1c[:, :], bo1.rearrange("(p a) -> p a", a=1))
            load(wo2[0:DM, :], Wo2)
            load(wo2[DM:DM + 1, :], bo2.rearrange("(a e) -> a e", a=1))
            for c in range(DC):
                load(kmix[:, c, :], mix[:, c * P:(c + 1) * P].rearrange("j p -> p j"), columns=True)
            load(gamma_b[:, :], gamma.partition_broadcast(P))
            load(beta_b[:, :], beta.partition_broadcast(P))
            load(bo_b[:, :], bo.partition_broadcast(P))
            w2_f = W2.rearrange("e m d -> (e m) d")
            w2_v = w2_s.rearrange("p (c d) -> p c d", c=HC)
            sp.wait_ge(w2_cleared, 1)
            load(w2_v[0:NP, 0, :], b2)
            load(w2_v[DM:P, 0, :], w2_f[0:DM, :])
            load(w2_v[:, 1:, :], w2_f[DM:, :].rearrange("(c p) d -> p c d", p=P))
            barrier(sp, 1)

            def ffn(ph, b, src, dst):
                g0 = seq(ph, b)
                for i in range(NT):
                    if i >= 4:
                        sp.wait_ge(x_in[i % 4], 4 * g0 + 16)
                    sp.dma_start(rows4(cols(X, i * SUB * D, SUB * D)), dram_tile(src, b * NT + i))\
                        .then_inc(x_in[i % 4], 16)
                with sp.Fori(0, NT) as t:
                    sp.wait_ge(x1_done, g0 + t + 2)
                    sp.dma_start(dram_tile(dst, b * NT + t), rows4(cols(N, t * SUB * D, SUB * D)))\
                        .then_inc(stored, 16)
                wait_apart(sp, stored, 16 * g0 + 16 * NT)

            def attention(b):
                with sp.Fori(0, NT) as j:
                    s = b * NT + j
                    sp.wait_ge(x2_stored, 16 * s + 1)
                    sp.dma_start(rows4(xr), dram_tile(x1_t, s)).then_inc(xr_in, 16)
                    sp.wait_ge(x2_done, SUB * s + SUB)
                    sp.dma_start(dram_tile(x2_t, s), rows4(xr)).then_inc(x2_stored, 16)
                wait_apart(sp, x2_stored, 16 * NT * b + 16 * NT + 1)

            sp.sem_inc(x2_stored, 1)
            with sp.Fori(0, B) as b:
                ffn(0, b, x_t, x1_t)
                barrier(sp, after_ffn(0, b))
                barrier(sp, after_ffn(0, b) + 1)
                attention(b)
                barrier(sp, after_ffn(0, b) + 2)
            with sp.Fori(0, B) as b:
                ffn(1, b, x2_t, out_t)
                barrier(sp, after_ffn(1, b))

        @block.gpsimd
        def _(pool):
            g = nc.gpsimd
            g.memset(th[DM:DM + 1, :], 1.0).then_inc(pool_const, 1)
            pool.wait_ge(pool_const, 1)
            g.memset(ident[:, :], 0.0).then_inc(pool_const, 1)
            g.memset(tri[:, :], 0.0).then_inc(pool_const, 1)
            g.memset(expand[:, :, :], 1.0).then_inc(pool_const, 1)
            g.memset(half[:, :], -0.5).then_inc(pool_const, 1)
            for e in range(NP):
                g.memset(prio[:, :, e:e + 1], float(NP - e)).then_inc(pool_const, 1)
            pool.wait_ge(pool_const, NP + 5)
            g.affine_select(out=ident[:, :], in_=ident[:, :], compare_op=ALU.not_equal, fill=1.0,
                            base=0, pattern=[[-1, P]], channel_multiplier=1).then_inc(pool_const, 1)
            g.affine_select(out=tri[:, :], in_=tri[:, :], compare_op=ALU.is_ge, fill=MASKED,
                            base=0, pattern=[[1, P]], channel_multiplier=-1).then_inc(pool_const, 1)
            expand_v = expand[:, :, :].rearrange("e c (k m) -> e (c k) m", m=DM)
            g.affine_select(out=expand_v, in_=expand_v, compare_op=ALU.is_equal, fill=0.0, base=-1,
                            pattern=[[1, 2 * HC], [0, DM]], channel_multiplier=-1).then_inc(pool_const, 1)
            pool.wait_ge(pool_const, NP + 8)
            g.affine_select(out=expand[:, 0, 0:DM], in_=expand[:, 0, 0:DM], compare_op=ALU.not_equal, fill=1.0,
                            base=0, pattern=[[-1, DM]], channel_multiplier=1).then_inc(pool_const, 1)
            barrier(pool, 1)

            def inverse_root(var_ready, eps_done, rstd_done, i, value, scale=1.0):
                wait_apart(pool, var_ready, value)
                g.tensor_scalar(veps[:, i, :], mv[:, i, :, 1], scale ** -2, EPS * scale ** -2, ALU.mult, ALU.add)\
                    .then_inc(eps_done, 1)
                pool.wait_ge(eps_done, value)
                g.tensor_tensor(rstd[:, i, :], veps[:, i, :], half[:, :], ALU.pow).then_inc(rstd_done, 1)

            def ffn(ph, b):
                g0 = seq(ph, b)
                with pool.Fori(0, NT // 2) as r:
                    for i in range(2):
                        inverse_root(n_var, n_eps, n_rstd, i, g0 + 2 * r + i + 1)
                with pool.Fori(0, NT) as t:
                    pool.wait_ge(x1_done, g0 + t + 1)
                    g.tensor_tensor(rows4(xb), rows4(cols(X, t * SUB * D, SUB * D)),
                                    beta_b[:, :].unsqueeze(1).to_broadcast([P, SUB, D]), ALU.add)\
                        .then_inc(xb_done, 1)
                    inverse_root(r_var, r_eps, r_rstd, 0, g0 + t + 1)

            def attention_input(b):
                with pool.Fori(0, NT) as t:
                    inverse_root(a_var, a_eps, a_rstd, 0, b * NT + t + 1, scale=XS)

            def attention(b):
                with pool.Fori(0, NT) as j:
                    s = b * NT + j
                    pool.wait_ge(xr_in, 16 * s + 16)
                    g.tensor_tensor(rows4(xr), rows4(xr), bo_b[:, :].unsqueeze(1).to_broadcast([P, SUB, D]),
                                    ALU.add).then_inc(xr_bo, 1)

            with pool.Fori(0, B) as b:
                ffn(0, b)
                barrier(pool, after_ffn(0, b))
                attention_input(b)
                barrier(pool, after_ffn(0, b) + 1)
                attention(b)
                barrier(pool, after_ffn(0, b) + 2)
            with pool.Fori(0, B) as b:
                ffn(1, b)
                barrier(pool, after_ffn(1, b))

        @block.vector
        def _(dve):
            v = nc.vector
            v.memset(w2_s[:, 0:D], 0.0).then_inc(w2_cleared, 1)
            dve.wait_ge(weights_in, 16 * LOADS)
            v.tensor_reduce(off_s[:, 0:3 * DC], wqkv_s.rearrange("p (i d) -> p i d", d=D), AX.X, ALU.add)
            v.tensor_scalar(bqkv_s[:, 0:3 * DC], bqkv_s[:, 0:3 * DC], 1.0 / (D * BETA), None, ALU.mult)\
                .then_inc(fold_step, 1)
            dve.wait_ge(fold_step, 1)
            v.scalar_tensor_tensor(out=off_s[:, 0:3 * DC], in0=off_s[:, 0:3 * DC], scalar=-1.0 / D,
                                   in1=bqkv_s[:, 0:3 * DC], op0=ALU.mult, op1=ALU.add).then_inc(fold_step, 1)
            dve.wait_ge(fold_step, 2)
            for i in range(3 * DC):
                v.tensor_scalar(cols(wqkv_s, i * D, D), cols(wqkv_s, i * D, D), off_s[:, i:i + 1], None, ALU.add)\
                    .then_inc(folded, 1)
            w1h, w1l, w2h, w2l = (a[:, :, :].rearrange("p a b -> p (a b)") for a in (w1_hi, w1_lo, w2_hi, w2_lo))
            v.tensor_scalar(w1h, w1_s, WS, None, ALU.mult)
            v.tensor_scalar(w2h, w2_s, WS, None, ALU.mult).then_inc(fold_step, 1)
            dve.wait_ge(fold_step, 3)
            v.scalar_tensor_tensor(out=w1l, in0=w1_s, scalar=WS, in1=w1h, op0=ALU.mult, op1=ALU.subtract)
            v.scalar_tensor_tensor(out=w2l, in0=w2_s, scalar=WS, in1=w2h, op0=ALU.mult, op1=ALU.subtract)
            v.tensor_scalar(b1c[:, 1:HC], b1_s[:, 1:HC], XS, None, ALU.mult)
            v.tensor_scalar(b1c[DM:P, 0:1], b1_s[DM:P, 0:1], XS, None, ALU.mult)
            v.tensor_scalar(kmix[:, :, :], kmix[:, :, :], XS, None, ALU.mult)
            v.tensor_scalar(gamma_b[:, :], gamma_b[:, :], 0.5, None, ALU.mult)
            v.tensor_scalar(beta_b[:, :], beta_b[:, :], 0.5, None, ALU.mult)
            v.memset(wvo[:, :, D:D + 8], 1.0 / (D * BETA))
            dve.wait_ge(pool_const, POOL_CONSTS)
            v.tensor_copy(ident16[:, :], ident[:, :])
            dve.wait_ge(woT_psum, 1)
            v.tensor_copy(wo_t, PS[:, 2, :]).then_inc(woT_done, 1)
            dve.wait_ge(wqk_psum, 1)
            for c in range(DC):
                v.tensor_scalar(wqk_hi[:, c, :], PS[:, c, 0:D], WS, None, ALU.mult).then_inc(fold_step, 1)
            dve.wait_ge(fold_step, 3 + DC)
            for c in range(DC):
                v.scalar_tensor_tensor(out=wqk_lo[:, c, :], in0=PS[:, c, 0:D], scalar=WS, in1=wqk_hi[:, c, :],
                                       op0=ALU.mult, op1=ALU.subtract)
            dve.wait_ge(wvo_psum, 1)
            for c in range(DC):
                v.tensor_copy(wvo[:, c, 0:D], PS[:, 3 + c, 0:D])
            dve.sem_inc(x1_done, 1)
            dve.sem_inc(y_done, 2)
            dve.sem_inc(hm_done, 2)
            dve.sem_inc(aT_lo, DC)
            dve.sem_inc(plo_done, 2)
            dve.sem_inc(spare_free[0], 1)
            dve.sem_inc(spare_free[1], 1)
            barrier(dve, 1)

            def row_stats(src, at, i, stat_done, var_done, value):
                for u in range(SUB):
                    ins = v.bn_stats(st[:, i, u, :], cols(src, at + u * D, D))
                ins.then_inc(stat_done, 1)
                wait_apart(dve, stat_done, value)
                for u in range(SUB):
                    ins = v.bn_aggr(mv[:, i, u, :], st[:, i, u, :])
                ins.then_inc(var_done, 1)

            def ffn(ph, b):
                g0 = seq(ph, b)
                nT_v = nT.rearrange("p (c s) -> p c s", c=DC)
                v.memset(nT_v[:, :, 0:1], 0.0)
                v.memset(nT_v[:, :, S + 1:S + 2], 0.0)
                v.memset(hb[0:DM, 0:TT], XS).then_inc(edges_set, 1)

                def normalise(t, i):
                    dve.wait_ge(n_rstd, g0 + t + 1)
                    dve.wait_ge(n_kept, g0 + t + 1)
                    for u in range(SUB):
                        ins = v.tensor_scalar(cols(Ns, (i % 2) * SUB * D + u * D, D), cols(X, t * SUB * D + u * D, D),
                                              mv[:, i % 2, u, 0:1], rstd[:, i % 2, u:u + 1], ALU.subtract, ALU.mult)
                    ins.then_inc(n_done, 1)

                with dve.Fori(0, NT // 4) as r:
                    for i in range(4):
                        t = 4 * r + i
                        dve.wait_ge(x_in[i], 4 * g0 + 16 * r + 16)
                        row_stats(X, t * SUB * D, i % 2, n_stat, n_var, g0 + t + 1)
                        if i >= 1:
                            normalise(t - 1, i - 1)
                    normalise(4 * r + 3, 3)
                dve.wait_ge(nT_done, DC * (g0 + NT) + DC)
                dve.wait_ge(edges_set, (ph * B + b) + 1)

                def mixed(t):
                    k = DC * (g0 + t)
                    for c in range(DC):
                        xm_c, at = cols(xm, c * TT, TT), c * NTC + t * TT
                        dve.wait_ge(xa_done, k + c + 1)
                        v.scalar_tensor_tensor(out=xm_c, in0=cols(nT, at, TT), scalar=kmix[:, c, 0:1],
                                               in1=cols(xa, c * TT, TT), op0=ALU.mult, op1=ALU.add)\
                            .then_inc(mix_part, 1)
                        dve.wait_ge(mix_part, k + c + 1)
                        v.scalar_tensor_tensor(out=xm_c, in0=cols(nT, at + 2, TT), scalar=kmix[:, c, 2:3],
                                               in1=xm_c, op0=ALU.mult, op1=ALU.add).then_inc(mix_done, 1)
                    for c in range(DC):
                        dve.wait_ge(xhi_done, k + c + 1)
                        v.tensor_tensor(cols(xlo, c * TT, TT), cols(xm, c * TT, TT), cols(xhi, c * TT, TT),
                                        ALU.subtract).then_inc(xlo_done, 1)

                def result_stats(t):
                    dve.wait_ge(o_psum, g0 + t + 1)
                    for i in range(2):
                        v.scalar_tensor_tensor(out=cols(y, i * TT, TT), in0=ps_o[:, i, :], scalar=1.0 / (XS * WS),
                                               in1=cols(N, t * SUB * D + i * TT, TT), op0=ALU.mult, op1=ALU.add)\
                            .then_inc(y_done, 1)
                    dve.wait_ge(y_done, 2 * (g0 + t) + 4)
                    row_stats(y, 0, 0, r_stat, r_var, g0 + t + 1)

                def result(t):
                    dve.wait_ge(r_rstd, g0 + t + 1)
                    for u in range(SUB):
                        ins = v.scalar_tensor_tensor(out=cols(z, u * D, D), in0=cols(y, u * D, D),
                                                     scalar=mv[:, 0, u, 0:1], in1=gamma_b[:, :],
                                                     op0=ALU.subtract, op1=ALU.mult)
                    ins.then_inc(r_mid, 1)
                    dve.wait_ge(r_mid, g0 + t + 1)
                    dve.wait_ge(xb_done, g0 + t + 1)
                    for u in range(SUB):
                        ins = v.scalar_tensor_tensor(out=cols(N, t * SUB * D + u * D, D), in0=cols(z, u * D, D),
                                                     scalar=rstd[:, 0, u:u + 1], in1=cols(xb, u * D, D),
                                                     op0=ALU.mult, op1=ALU.add)
                    ins.then_inc(x1_done, 1)

                def route(t):
                    k = 4 * (g0 + t)
                    dve.wait_ge(route_psum, g0 + t + 1)
                    v.tensor_reduce(r_max[:, :], ps_route, AX.X, ALU.max).then_inc(route_step, 1)
                    dve.wait_ge(route_step, k + 1)
                    v.tensor_tensor(r_eq[:, :, :], ps_route, r_max[:, :].unsqueeze(2).to_broadcast([P, SUB, NP]),
                                    ALU.is_equal).then_inc(route_step, 1)
                    dve.wait_ge(route_step, k + 2)
                    v.tensor_tensor(r_pr[:, :, :], r_eq[:, :, :], prio[:, :, :], ALU.mult).then_inc(route_step, 1)
                    dve.wait_ge(route_step, k + 3)
                    v.tensor_reduce(r_top[:, :], r_pr[:, :, :], AX.X, ALU.max).then_inc(route_step, 1)
                    dve.wait_ge(route_step, k + 4)
                    v.tensor_tensor(oh[:, :, :], r_pr[:, :, :], r_top[:, :].unsqueeze(2).to_broadcast([P, SUB, NP]),
                                    ALU.is_equal).then_inc(oh_done, 1)

                def chosen(t):
                    k = HC * (g0 + t)

                    def low(c):
                        dve.wait_ge(hhi_done, k + c + 1)
                        v.tensor_tensor(cols(hlo, c * TT, TT), cols(hm, (c % 2) * TT, TT), cols(hhi, c * TT, TT),
                                        ALU.subtract).then_inc(hlo_done, 1)

                    for c in range(HC):
                        dve.wait_ge(hb_done, k + c + 3)
                        dve.wait_ge(mask_psum, k + c + 1)
                        v.tensor_tensor(cols(hm, (c % 2) * TT, TT), ps_m[:, c % 2, :], cols(hb, c * TT, TT), ALU.mult)\
                            .then_inc(hm_done, 1)
                        if c >= 1:
                            low(c - 1)
                    low(HC - 1)

                mixed(0)

                def tile(t, first, last):
                    if not first:
                        result_stats(t - 1)
                    route(t)
                    if not first:
                        result(t - 1)
                    chosen(t)
                    if not last:
                        mixed(t + 1)

                over_tiles(dve, tile)
                result_stats(NT - 1)
                result(NT - 1)

            def attention_input(b):
                def normalise(t):
                    dve.wait_ge(a_rstd, b * NT + t + 1)
                    for u in range(SUB):
                        ins = v.tensor_scalar(cols(Ns, (t & 1) * SUB * D + u * D, D), cols(N, t * SUB * D + u * D, D), mv[:, 0, u, 0:1], rstd[:, 0, u:u + 1],
                                              ALU.subtract, ALU.mult)
                    ins.then_inc(a_done, 1)

                def stats(t):
                    row_stats(N, t * SUB * D, 0, a_stat, a_var, b * NT + t + 1)

                def lows(t):
                    dve.wait_ge(a_hi, b * NT + t + 1)
                    v.scalar_tensor_tensor(out=cols(KV_lo, t * SUB * D, SUB * D), in0=cols(Ns, (t & 1) * SUB * D, SUB * D),
                                           scalar=XS * BETA, in1=cols(KV_hi, t * SUB * D, SUB * D),
                                           op0=ALU.add, op1=ALU.subtract)
                    for c in range(DC):
                        dve.wait_ge(aT_hi, DC * (b * NT + t) + c + 1)
                        v.scalar_tensor_tensor(out=cols(KT_lo, c * S + t * TT, TT), in0=ps_o[:, c, :],
                                               scalar=XS * BETA, in1=cols(KT_hi, c * S + t * TT, TT),
                                               op0=ALU.add, op1=ALU.subtract).then_inc(aT_lo, 1)

                for t in range(2):
                    stats(t)
                    normalise(t)
                with dve.Fori(0, NT - 2) as t:
                    stats(t + 2)
                    lows(t)
                    dve.wait_ge(aT_lo, DC * (b * NT + t) + 2 * DC)
                    normalise(t + 2)
                lows(NT - 2)
                lows(NT - 1)

            def attention(b):
                def q_low(j, k):
                    for c in range(DC):
                        dve.wait_ge(q_hi_done, DC * (b * NT + j) + c + 1)
                        at = (j & 1) * (DC * TT) + c * TT
                        v.scalar_tensor_tensor(out=cols(q_lo, at, TT), in0=ps_x[:, c, :], scalar=QS / (XS * WS),
                                               in1=cols(q_hi, at, TT), op0=ALU.mult, op1=ALU.subtract)\
                            .then_inc(spare_free[c], 1)

                def score_max(j, m, i, diagonal, before, ring_m):
                    n = before + i
                    lo = i * P if diagonal else 0
                    at = ring_m + i * TT + lo
                    dve.wait_ge(abs_done, n + SUB + 1)
                    if diagonal:
                        v.tensor_tensor(cols(ring, at, P), cols(ring, at, P), tri[:, :], ALU.add)\
                            .then_inc(tri_done, 1)
                        dve.wait_ge(tri_done, SUB * (b * NT + j) + i + 1)
                    if isinstance(m, int) and m == 0 and i == 0:
                        v.tensor_copy(run_max[:, :], cols(ring, at, TT)).then_inc(max_done, 1)
                    else:
                        dve.wait_ge(max_done, n)
                        v.tensor_tensor(run_max[:, lo:], run_max[:, lo:], cols(ring, at, TT - lo), ALU.max)\
                            .then_inc(max_done, 1)

                def shifted(i, diagonal, ring_n):
                    lo = i * P if diagonal else 0
                    at = ring_n + i * TT + lo
                    v.tensor_tensor(cols(ring, at, TT - lo), cols(ring, at, TT - lo), max_row[:, lo:], ALU.subtract)\
                        .then_inc(sub_done, 1)

                def p_low(i, diagonal, before):
                    lo = i * P if diagonal else 0
                    dve.wait_ge(phi_done, before + i + 1)
                    v.tensor_tensor(p_lo[:, i * TT + lo:(i + 1) * TT], pf[:, (i % 2) * TT + lo:(i % 2 + 1) * TT],
                                    p_hi[:, i * TT + lo:(i + 1) * TT], ALU.subtract).then_inc(plo_done, 1)

                def output(j):
                    s = b * NT + j
                    dve.wait_ge(xr_bo, s + 1)
                    for u in range(SUB):
                        dve.wait_ge(out_psum, SUB * s + u + 1)
                        v.reciprocal(rden[:, u:u + 1], ps_x[:, u % 2, D:D + 1]).then_inc(rden_done, 1)
                        dve.wait_ge(rden_done, SUB * s + u + 1)
                        v.scalar_tensor_tensor(out=cols(xr, u * D, D), in0=ps_x[:, u % 2, 0:D],
                                               scalar=rden[:, u:u + 1], in1=cols(xr, u * D, D),
                                               op0=ALU.mult, op1=ALU.add).then_inc(x2_done, 1)

                def step(j):
                    k = b * SPARE + spare(j)
                    if has_q(j):
                        q_low(j + 2, k)
                        k = k + 1
                    if has_o(j):
                        output(j - 1)
                    dve.wait_ge(maxT_psum, b * NT + j + 1)
                    v.tensor_reduce(max_col[:, :], rows4(ps_x[:, 0, :]), AX.X, ALU.max).then_inc(spare_free[0], 1)

                    def pair(m, a_diagonal, b_diagonal, with_a, with_b):
                        if with_a:
                            a_before, a_ring = blocks(dve, b, j + 1, m), ring_at(dve, j + 1, m)
                        if with_b:
                            b_before, b_ring = blocks(dve, b, j, m), ring_at(dve, j, keys_at(dve, j, m))
                        for i in range(SUB):
                            if with_a:
                                score_max(j + 1, m, i, a_diagonal, a_before, a_ring)
                            if with_b:
                                if b_diagonal and i == 0:
                                    dve.wait_ge(spare_free[1], k + 2)
                                shifted(i, b_diagonal, b_ring)
                                if i >= 1:
                                    p_low(i - 1, b_diagonal, b_before)
                        if with_b:
                            p_low(SUB - 1, b_diagonal, b_before)

                    more = not (isinstance(j, int) and j == NT - 1)
                    none = isinstance(j, int) and j == 0
                    pair(0, False, True, more, True)
                    if not none:
                        with dve.Fori(1, j + 1) as m:
                            pair(m, False, False, more, True)
                    if more:
                        pair(j + 1, True, False, True, False)

                q_low(0, 0)
                q_low(1, 1)
                before = blocks(dve, b, 0, 0)
                for i in range(SUB):
                    score_max(0, 0, i, True, before, ring_at(dve, 0, 0))
                over_steps(dve, step, step, step)
                output(NT - 1)

            with dve.Fori(0, B) as b:
                ffn(0, b)
                barrier(dve, after_ffn(0, b))
                attention_input(b)
                barrier(dve, after_ffn(0, b) + 1)
                attention(b)
                barrier(dve, after_ffn(0, b) + 2)
            with dve.Fori(0, B) as b:
                ffn(1, b)
                barrier(dve, after_ffn(1, b))

        @block.scalar
        def _(act):
            a = nc.scalar
            act.sem_inc(nT_done, DC)
            act.sem_inc(n_kept, 2)
            act.sem_inc(hb_done, 2)
            act.sem_inc(abs_done, SUB)
            act.sem_inc(u_done, 1)
            barrier(act, 1)

            def ffn(ph, b):
                g0 = seq(ph, b)
                with act.Fori(0, NT) as t:
                    for c in range(DC):
                        act.wait_ge(nT_psum, DC * (g0 + t) + c + 1)
                        a.activation(cols(nT, c * NTC + t * TT + 1, TT), ps_o[:, c, :], ACT.Copy).then_inc(nT_done, 1)
                    act.wait_ge(n_done, g0 + t + 1)
                    a.activation(cols(N, t * SUB * D, SUB * D), cols(Ns, (t & 1) * SUB * D, SUB * D), ACT.Copy)\
                        .then_inc(n_kept, 1)
                act.wait_ge(nT_done, DC * (g0 + NT) + DC)

                def middle(t):
                    for c in range(DC):
                        a.activation(cols(xa, c * TT, TT), cols(nT, c * NTC + t * TT + 1, TT), ACT.Copy,
                                     scale=kmix[:, c, 1:2]).then_inc(xa_done, 1)

                def x_high(t):
                    for c in range(DC):
                        act.wait_ge(mix_done, DC * (g0 + t) + c + 1)
                        a.activation(cols(xhi, c * TT, TT), cols(xm, c * TT, TT), ACT.Copy).then_inc(xhi_done, 1)

                middle(0)
                x_high(0)

                def tile(t, first, last):
                    k = HC * (g0 + t)
                    act.wait_ge(h_psum, k + 1)
                    a.activation(th[0:DM, :], ps_h[0:DM, 0, :], ACT.Tanh, bias=bo1c[:, :], scale=1.0 / (XS * WS))\
                        .then_inc(tanh_done, 1)
                    act.wait_ge(hm_done, k + 2)
                    a.activation(hb[DM:P, 0:TT], ps_h[DM:P, 0, :], ACT.Identity, bias=b1c[DM:P, 0:1], scale=1.0 / WS)\
                        .then_inc(hb_done, 1)
                    for c in range(1, HC):
                        if c == HC - 1:
                            act.wait_ge(ohT_psum, g0 + t + 1)
                            a.activation(oh_t[:, :], ps_oh[0:NP, 0:TT], ACT.Copy).then_inc(ohT_done, 1)
                        act.wait_ge(h_psum, k + c + 1)
                        a.activation(cols(hb, c * TT, TT), ps_h[:, c % 2, :], ACT.Identity, bias=b1c[:, c:c + 1],
                                     scale=1.0 / WS).then_inc(hb_done, 1)
                    if not last:
                        middle(t + 1)
                    for c in range(HC):
                        act.wait_ge(hm_done, k + c + 3)
                        if c == 0 and not first:
                            act.wait_ge(o_psum, g0 + t)
                        a.activation(cols(hhi, c * TT, TT), cols(hm, (c % 2) * TT, TT), ACT.Copy).then_inc(hhi_done, 1)
                    if not last:
                        act.wait_ge(h_psum, k + HC)
                        x_high(t + 1)

                over_tiles(act, tile)

            def attention_input(b):
                with act.Fori(0, NT) as t:
                    g = b * NT + t
                    act.wait_ge(a_done, g + 1)
                    a.activation(cols(KV_hi, t * SUB * D, SUB * D), cols(Ns, (t & 1) * SUB * D, SUB * D), ACT.Copy,
                                 bias=XS * BETA).then_inc(a_hi, 1)
                    for c in range(DC):
                        act.wait_ge(aT_psum, DC * g + c + 1)
                        a.activation(cols(KT_hi, c * S + t * TT, TT), ps_o[:, c, :], ACT.Copy, bias=XS * BETA)\
                            .then_inc(aT_hi, 1)

            def attention(b):
                def q_high(j):
                    for c in range(DC):
                        act.wait_ge(q_psum, DC * (b * NT + j) + c + 1)
                        a.activation(cols(q_hi, (j & 1) * (DC * TT) + c * TT, TT), ps_x[:, c, :], ACT.Copy,
                                     scale=QS / (XS * WS)).then_inc(q_hi_done, 1)

                def absolute(i, diagonal, before, ring_m):
                    lo = i * P if diagonal else 0
                    act.wait_ge(s_psum, before + i + 1)
                    a.activation(cols(ring, ring_m + i * TT + lo, TT - lo), ps_s[:, i, lo:], ACT.Abs,
                                 scale=1.0 / (QS * XS * D ** 0.5)).then_inc(abs_done, 1)

                def probability(i, diagonal, before, ring_n):
                    lo = i * P if diagonal else 0
                    k = before + i
                    p = pf[:, (i % 2) * TT + lo:(i % 2 + 1) * TT]
                    act.wait_ge(plo_done, k + 1)
                    act.wait_ge(sub_done, k + 1)
                    a.activation(p, cols(ring, ring_n + i * TT + lo, TT - lo), ACT.Exp)\
                        .then_inc(exp_done, 1)
                    act.wait_ge(pv_done, k + 1)
                    act.wait_ge(exp_done, k + 1)
                    a.activation(p_hi[:, i * TT + lo:(i + 1) * TT], p, ACT.Copy).then_inc(phi_done, 1)

                def weighted(j):
                    s = b * NT + j
                    act.wait_ge(pv_done, blocks(act, b, j + 1, 0) + SUB)
                    a.activation(U[:, 0:TT], ps_u[:, 0, :], ACT.Copy)
                    a.activation(U[:, TT:], ps_u[:, 1, :], ACT.Copy).then_inc(u_done, 1)

                def step(j):
                    if has_q(j):
                        q_high(j + 2)
                    if has_o(j):
                        weighted(j - 1)
                    act.wait_ge(maxrow_psum, b * NT + j + 1)
                    a.activation(max_row[:, :], ps_x[:, 1, :], ACT.Copy, bias=-P_LOG).then_inc(spare_free[1], 1)

                    def pair(m, a_diagonal, b_diagonal, with_a, with_b):
                        if with_a:
                            a_before, a_ring = blocks(act, b, j + 1, m), ring_at(act, j + 1, m)
                        if with_b:
                            b_before, b_ring = blocks(act, b, j, m), ring_at(act, j, keys_at(act, j, m))
                        for i in range(SUB):
                            if with_a:
                                absolute(i, a_diagonal, a_before, a_ring)
                            if with_b:
                                probability(i, b_diagonal, b_before, b_ring)

                    more = not (isinstance(j, int) and j == NT - 1)
                    pair(0, False, True, more, True)
                    if not (isinstance(j, int) and j == 0):
                        with act.Fori(1, j + 1) as m:
                            pair(m, False, False, more, True)
                    if more:
                        pair(j + 1, True, False, True, False)

                q_high(0)
                q_high(1)
                before = blocks(act, b, 0, 0)
                for i in range(SUB):
                    absolute(i, True, before, ring_at(act, 0, 0))
                over_steps(act, step, step, step)
                weighted(NT - 1)

            with act.Fori(0, B) as b:
                ffn(0, b)
                barrier(act, after_ffn(0, b))
                attention_input(b)
                barrier(act, after_ffn(0, b) + 1)
                attention(b)
                barrier(act, after_ffn(0, b) + 2)
            with act.Fori(0, B) as b:
                ffn(1, b)
                barrier(act, after_ffn(1, b))

        @block.tensor
        def _(pe):
            t_ = nc.tensor

            def split_product(dst, pairs, start, stop, skip=False):
                last = 3 * len(pairs) - 1
                n = 0
                for (w_h, w_l), (x_h, x_l) in pairs:
                    for w, xx in ((w_h, x_h), (w_h, x_l), (w_l, x_h)):
                        ins = t_.matmul(dst, w, xx, start=start and n == 0, stop=stop and n == last,
                                        skip_group_check=skip)
                        n += 1
                return ins

            def transpose_rows(i, c):
                for u in range(SUB):
                    ins = t_.transpose(ps_o[:, c, u * P:(u + 1) * P], cols(Ns, (i * SUB + u) * D + c * P, P), ident[:, :])
                return ins

            pe.sem_inc(pv_done, SUB)
            pe.wait_ge(weights_in, 16 * LOADS)
            pe.wait_ge(pool_const, POOL_CONSTS)
            for c in range(DC):
                for d in range(DC):
                    ins = t_.transpose(PS[:, 2, d * D + c * P:d * D + (c + 1) * P],
                                       wo_s[:, c * D + d * P:c * D + (d + 1) * P], ident[:, :])
            ins.then_inc(woT_psum, 1)
            pe.wait_ge(folded, 3 * DC)
            wq_f, wk_f, wv_f = (wqkv_s[:, i * DC * D:(i + 1) * DC * D] for i in range(3))
            for d in range(DC):
                for c in range(DC):
                    ins = t_.matmul(PS[:, d, 0:D], wq_f[:, c * D + d * P:c * D + (d + 1) * P],
                                    wk_f[:, c * D:(c + 1) * D], start=c == 0, stop=c == DC - 1)
            ins.then_inc(wqk_psum, 1)
            pe.wait_ge(woT_done, 1)
            for d in range(DC):
                for c in range(DC):
                    ins = t_.matmul(PS[:, 3 + d, 0:D], wv_f[:, c * D + d * P:c * D + (d + 1) * P],
                                    wo_t[:, c * D:(c + 1) * D], start=c == 0, stop=c == DC - 1)
            ins.then_inc(wvo_psum, 1)
            barrier(pe, 1)

            def ffn(ph, b):
                g0 = seq(ph, b)
                with pe.Fori(0, NT // 2) as r:
                    for i in range(2):
                        g = g0 + 2 * r + i
                        pe.wait_ge(n_done, g + 1)
                        for c in range(DC):
                            pe.wait_ge(nT_done, DC * g + c + 1)
                            transpose_rows(i, c).then_inc(nT_psum, 1)

                def tile(t, first, last):
                    g = g0 + t
                    k = HC * g

                    def hidden(c):
                        pe.wait_ge(hb_done, k + c + 1 if c >= 2 else k + 2)
                        split_product(ps_h[:, c % 2, :],
                                      [((w1_hi[:, d, c * P:(c + 1) * P], w1_lo[:, d, c * P:(c + 1) * P]),
                                        (cols(xhi, d * TT, TT), cols(xlo, d * TT, TT))) for d in range(DC)],
                                      True, True).then_inc(h_psum, 1)

                    def mask(c):
                        pe.wait_ge(hm_done, k + c + 1 if c >= 2 else k + 2)
                        t_.matmul(ps_m[:, c % 2, :], expand[:, c, :], oh_t[:, :], start=True, stop=True)\
                            .then_inc(mask_psum, 1)

                    def path(c):
                        pe.wait_ge(hlo_done, k + c + 1)
                        for u in range(SUB):
                            at = c * TT + u * P
                            ins = split_product(ps_o[:, u // 2, (u % 2) * D:(u % 2 + 1) * D],
                                                [((cols(hhi, at, P), cols(hlo, at, P)),
                                                  (w2_hi[:, c, :], w2_lo[:, c, :]))],
                                                c == 0 and u % 2 == 0, c == HC - 1, skip=True)
                        if c == HC - 1:
                            ins.then_inc(o_psum, 1)

                    pe.wait_ge(xlo_done, DC * g + DC)
                    hidden(0)
                    hidden(1)
                    pe.wait_ge(tanh_done, g + 1)
                    for u in range(SUB):
                        ins = t_.matmul(ps_route[:, u, :], th[:, u * P:(u + 1) * P], wo2[:, :], start=True, stop=True)
                    ins.then_inc(route_psum, 1)
                    hidden(2)
                    hidden(3)
                    pe.wait_ge(oh_done, g + 1)
                    for u in range(SUB):
                        ins = t_.transpose(ps_oh[0:NP, u * P:(u + 1) * P], oh[:, u, :], ident16[:, :])
                    ins.then_inc(ohT_psum, 1)
                    hidden(4)
                    pe.wait_ge(ohT_done, g + 1)
                    mask(0)
                    mask(1)
                    pe.wait_ge(y_done, 2 * g + 2)
                    for c in range(HC):
                        path(c)
                        if c + 2 < HC:
                            mask(c + 2)

                over_tiles(pe, tile)

            def attention_input(b):
                with pe.Fori(0, NT // 2) as r:
                    for i in range(2):
                        g = b * NT + 2 * r + i
                        pe.wait_ge(a_done, g + 1)
                        for c in range(DC):
                            pe.wait_ge(aT_lo, DC * g + c + 1)
                            transpose_rows(i, c).then_inc(aT_psum, 1)

            def attention(b):
                def queries(j, k):
                    for c in range(DC):
                        pe.wait_ge(spare_free[c], k + 1)
                        split_product(ps_x[:, c, :],
                                      [((wqk_hi[:, d, c * P:(c + 1) * P], wqk_lo[:, d, c * P:(c + 1) * P]),
                                        (cols(KT_hi, d * S + j * TT, TT), cols(KT_lo, d * S + j * TT, TT)))
                                       for d in range(DC)], True, True).then_inc(q_psum, 1)

                def scores(j, m, diagonal):
                    before = blocks(pe, b, j, m)
                    for i in range(SUB):
                        lo = i * P if diagonal else 0
                        pe.wait_ge(abs_done, before + i + 1)
                        at = m * TT + i * P
                        q_at = (j & 1) * (DC * TT) + lo
                        split_product(ps_s[:, i, lo:],
                                      [((cols(KT_hi, d * S + at, P), cols(KT_lo, d * S + at, P)),
                                        (cols(q_hi, q_at + d * TT, TT - lo), cols(q_lo, q_at + d * TT, TT - lo)))
                                       for d in range(DC)], True, True).then_inc(s_psum, 1)

                def values(j, n, diagonal):
                    before, keys = blocks(pe, b, j, n), keys_at(pe, j, n)
                    for i in range(SUB):
                        lo = i * P if diagonal else 0
                        pe.wait_ge(plo_done, before + i + 3)
                        at = (keys * SUB + i) * D
                        for c in range(DC):
                            ins = split_product(ps_u[:, c, lo:],
                                                [((cols(KV_hi, at + c * P, P), cols(KV_lo, at + c * P, P)),
                                                  (p_hi[:, i * TT + lo:(i + 1) * TT], p_lo[:, i * TT + lo:(i + 1) * TT]))],
                                                diagonal and i == 0, i == SUB - 1, skip=True)
                        ins.then_inc(pv_done, 1)

                def output(j, k):
                    s = b * NT + j
                    pe.wait_ge(u_done, s + 2)
                    for u in range(SUB):
                        if u < 2:
                            pe.wait_ge(spare_free[u], k + 1)
                        else:
                            pe.wait_ge(x2_done, SUB * s + u - 1)
                        for c in range(DC):
                            ins = t_.matmul(ps_x[:, u % 2, 0:D + 1], U[:, c * TT + u * P:c * TT + (u + 1) * P],
                                            wvo[:, c, 0:D + 1], start=c == 0, stop=c == DC - 1)
                        ins.then_inc(out_psum, 1)

                def step(j):
                    s = b * NT + j
                    k = b * SPARE + spare(j)
                    if has_q(j):
                        queries(j + 2, k)
                        k = k + 1
                    if has_o(j):
                        output(j - 1, k)
                        pe.wait_ge(x2_done, SUB * s)
                    pe.wait_ge(spare_free[0], k + 1)
                    pe.wait_ge(spare_free[1], k + 1)
                    pe.wait_ge(max_done, blocks(pe, b, j + 1, 0))
                    for u in range(SUB):
                        ins = t_.transpose(ps_x[:, 0, u * P:(u + 1) * P], run_max[:, u * P:(u + 1) * P], ident[:, :])
                    ins.then_inc(maxT_psum, 1)
                    pe.wait_ge(spare_free[0], k + 2)
                    for u in range(SUB):
                        ins = t_.transpose(ps_x[:, 1, u * P:(u + 1) * P], max_col[:, u:u + 1].to_broadcast([P, P]),
                                           ident[:, :])
                    ins.then_inc(maxrow_psum, 1)
                    more = not (isinstance(j, int) and j == NT - 1)
                    if more:
                        scores(j + 1, 0, False)
                    wait_apart(pe, u_done, s + 1)
                    values(j, 0, True)
                    if not (isinstance(j, int) and j == 0):
                        with pe.Fori(1, j + 1) as m:
                            if more:
                                scores(j + 1, m, False)
                            values(j, m, False)
                    if more:
                        scores(j + 1, j + 1, True)

                queries(0, b * SPARE)
                queries(1, b * SPARE + 1)
                scores(0, 0, True)
                over_steps(pe, step, step, step)
                output(NT - 1, b * SPARE + SPARE)

            with pe.Fori(0, B) as b:
                ffn(0, b)
                barrier(pe, after_ffn(0, b))
                attention_input(b)
                barrier(pe, after_ffn(0, b) + 1)
                attention(b)
                barrier(pe, after_ffn(0, b) + 2)
            with pe.Fori(0, B) as b:
                ffn(1, b)
                barrier(pe, after_ffn(1, b))


_INS = ["L0_attn_x", "L0_attn_Wq", "L0_attn_bq", "L0_attn_Wk", "L0_attn_bk", "L0_attn_Wv", "L0_attn_bv", "L0_attn_Wo",
        "L0_attn_bo", "L0_ffn_mix_kernel", "L0_ffn_W1", "L0_ffn_b1", "L0_ffn_W2", "L0_ffn_b2", "L0_ffn_Wo1",
        "L0_ffn_bo1", "L0_ffn_Wo2", "L0_ffn_bo2", "L0_ffn_gamma", "L0_ffn_beta"]


def kernel(**inputs):
    import numpy as _np
    import concourse.bacc as _bacc
    from concourse.bass_utils import run_bass_kernel_spmd as _run

    nc = _bacc.Bacc("TRN2", target_bir_lowering=False, num_devices=1)
    arrays, args = {}, []
    for name in _INS:
        a = _np.ascontiguousarray(inputs[name])
        arrays[f"in_{name}"] = a
        args.append(nc.dram_tensor(f"in_{name}", a.shape, mybir.dt.from_np(a.dtype), kind="ExternalInput").ap())
    out = nc.dram_tensor("out_0", (B, S, D), F32, kind="ExternalOutput").ap()
    macaron(nc, *args, out)
    r = _run(nc, [arrays], core_ids=[0])
    return r.results[0]["out_0"]
```

```python
import concourse.bass as bass
from concourse import mybir
from contextlib import ExitStack

F32 = mybir.dt.float32
F16 = mybir.dt.float16
ALU = mybir.AluOpType
ACT = mybir.ActivationFunctionType
AX = mybir.AxisListType

P = 128
B, S, D = 2, 4096, 256
NP, DM = 9, 64
DC = D // P
TT = 512
SUB = TT // P
NT = S // TT
HC = (DM + NP * DM) // P
EPS = 1e-5

XS = 64.0
WS = 64.0
QS = 32.0
BETA = 1.0 / 16
P_LOG = 8.317766166719343
MASKED = -1e30

RING = 10


def macaron(nc, x, Wq, bq, Wk, bk, Wv, bv, Wo, bo, mix, W1, b1, W2, b2, Wo1, bo1, Wo2, bo2,
            gamma, beta, out):
    x1 = nc.dram_tensor("x1_scratch", (B, S, D), F32, kind="Internal").ap()
    x2 = nc.dram_tensor("x2_scratch", (B, S, D), F32, kind="Internal").ap()

    def tiles(a):
        return a.rearrange("b (t u p) d -> (b t) p u d", u=SUB, p=P)

    x_t, x1_t, x2_t, out_t = tiles(x), tiles(x1), tiles(x2), tiles(out)

    ctx = ExitStack()
    with ctx:
        def sb(name, shape, dt=F32):
            return ctx.enter_context(nc.sbuf_tensor(name, shape, dt))

        def sem(name):
            return ctx.enter_context(nc.semaphore(name))

        R1 = sb("R1", [P, RING * SUB * TT])
        R2 = sb("R2", [P, 16384])
        R3 = sb("R3", [P, NT * SUB * D])

        class Region:

            def __init__(self, tensor):
                self.tensor, self.at = tensor, 0

            def take(self, n, dt=F32):
                words = n if dt == F32 else n // 2
                part = self.tensor[:, self.at:self.at + words]
                self.at += words
                assert self.at <= self.tensor.shape[1]
                return part if dt == F32 else part.bitcast(dt)

        f1, f2 = Region(R1), Region(R2)
        X = f1.take(NT * SUB * D)
        NTC = S + 2
        nT = f1.take(DC * NTC)
        Ns = f1.take(2 * SUB * D)
        N = R3[:, :]
        hb = f2.take(HC * TT)
        hm = f2.take(2 * TT)
        hhi = f2.take(HC * TT, F16)
        hlo = f2.take(HC * TT, F16)
        xa = f2.take(DC * TT)
        xm = f2.take(DC * TT)
        xhi = f2.take(2 * DC * TT, F16)
        xlo = f2.take(2 * DC * TT, F16)
        y = f2.take(SUB * D)
        z = f2.take(SUB * D)
        xb = f2.take(SUB * D)
        a1, a2, a3 = Region(R1), Region(R2), Region(R3)
        ring = a1.take(RING * SUB * TT)
        KT_hi = a2.take(DC * S, F16)
        KT_lo = a2.take(DC * S, F16)
        KV_hi = a2.take(S // P * D, F16)
        KV_lo = a2.take(S // P * D, F16)
        q_hi = a3.take(2 * DC * TT, F16)
        q_lo = a3.take(2 * DC * TT, F16)
        pf = a3.take(2 * TT)
        p_hi = a3.take(SUB * TT, F16)
        p_lo = a3.take(SUB * TT, F16)
        U = a3.take(DC * TT)
        xr = a3.take(SUB * D)

        run_max = sb("run_max", [P, TT])
        max_row = sb("max_row", [P, TT])
        max_col = sb("max_col", [P, SUB])
        rden = sb("rden", [P, SUB])
        w1_hi = sb("w1_hi", [P, DC, HC * P], F16)
        w1_lo = sb("w1_lo", [P, DC, HC * P], F16)
        w2_hi = sb("w2_hi", [P, HC, D], F16)
        w2_lo = sb("w2_lo", [P, HC, D], F16)
        wqk_hi = sb("wqk_hi", [P, DC, D], F16)
        wqk_lo = sb("wqk_lo", [P, DC, D], F16)
        wvo = sb("wvo", [P, DC, D + 8])
        wo2 = sb("wo2", [DM + 1, NP])
        b1c = sb("b1c", [P, HC])
        bo1c = sb("bo1c", [DM, 1])
        kmix = sb("kmix", [P, DC, 3])
        gamma_b = sb("gamma_b", [P, D])
        beta_b = sb("beta_b", [P, D])
        bo_b = sb("bo_b", [P, D])
        ident = sb("ident", [P, P])
        ident16 = sb("ident16", [P, P], F16)
        tri = sb("tri", [P, P])
        expand = sb("expand", [NP, HC, P], F16)
        prio = sb("prio", [P, SUB, NP])
        half = sb("half", [P, SUB])
        th = sb("th", [DM + 1, TT])
        oh = sb("oh", [P, SUB, NP], F16)
        oh_t = sb("oh_t", [NP, TT], F16)
        r_max = sb("r_max", [P, SUB])
        r_eq = sb("r_eq", [P, SUB, NP])
        r_pr = sb("r_pr", [P, SUB, NP])
        r_top = sb("r_top", [P, SUB])
        st = sb("st", [P, 2, SUB, 6])
        mv = sb("mv", [P, 2, SUB, 2])
        rstd = sb("rstd", [P, 2, SUB])
        veps = sb("veps", [P, 2, SUB])
        r_neg = sb("r_neg", [P, SUB])
        r_bias = sb("r_bias", [P, SUB])
        s1 = Region(R1)
        wqkv_s = s1.take(3 * DC * D)
        wo_s = s1.take(DC * D)
        wo_t = s1.take(DC * D)
        w1_s = s1.take(DC * HC * P)
        w2_s = s1.take(HC * D)
        bqkv_s = s1.take(8)
        off_s = s1.take(8)
        b1_s = s1.take(8)

        PS = ctx.enter_context(nc.psum_tensor("PS", [P, 8, TT], F32))
        ps_h, ps_m, ps_o, ps_r = PS[:, 0:2, :], PS[:, 2:4, :], PS[:, 4:6, :], PS[:, 6, :]
        ps_oh = PS[:, 7, :].bitcast(F16)
        ps_s, ps_u, ps_x = PS[:, 0:4, :], PS[:, 4:6, :], PS[:, 6:8, :]

        ps_route = ps_r[:, 0:SUB * 16].rearrange("p (u e) -> p u e", u=SUB)[:, :, 0:NP]

        waited = sem("waited")
        phase_done, weights_in, w2_cleared = sem("phase_done"), sem("weights_in"), sem("w2_cleared")
        pool_const, fold_step, folded, woT_psum = sem("pool_const"), sem("fold_step"), sem("folded"), sem("woT_psum")
        woT_done, wqk_psum, wvo_psum = sem("woT_done"), sem("wqk_psum"), sem("wvo_psum")
        x_in = [sem(f"x_in{i}") for i in range(4)]
        n_stat, n_var, n_eps, n_rstd, n_done, n_kept = (sem("n_" + s) for s in ("stat", "var", "eps", "rstd", "done", "kept"))
        r_stat, r_var, r_eps, r_rstd, r_mid = (sem("r_" + s) for s in ("stat", "var", "eps", "rstd", "mid"))
        r_neg_done, r_bias_done, z_done = sem("r_neg_done"), sem("r_bias_done"), sem("z_done")
        a_stat, a_var, a_eps, a_rstd, a_done = (sem("a_" + s) for s in ("stat", "var", "eps", "rstd", "done"))
        nT_psum, nT_done, edges_set = sem("nT_psum"), sem("nT_done"), sem("edges_set")
        xa_done, mix_part, mix_done = sem("xa_done"), sem("mix_part"), sem("mix_done")
        xhi_done, xlo_done = sem("xhi_done"), sem("xlo_done")
        h_psum, hb_done, tanh_done = sem("h_psum"), sem("hb_done"), sem("tanh_done")
        route_psum, route_step, oh_done = sem("route_psum"), sem("route_step"), sem("oh_done")
        ohT_psum, ohT_done, mask_psum = sem("ohT_psum"), sem("ohT_done"), sem("mask_psum")
        hm_done, hhi_done, hlo_done = sem("hm_done"), sem("hhi_done"), sem("hlo_done")
        o_psum, y_done, xb_done, x1_done, stored = (sem("o_psum"), sem("y_done"), sem("xb_done"), sem("x1_done"),
                                                    sem("stored"))
        a_hi, a_lo, aT_psum, aT_hi, aT_lo = sem("a_hi"), sem("a_lo"), sem("aT_psum"), sem("aT_hi"), sem("aT_lo")
        q_psum, q_hi_done, spare_free = sem("q_psum"), sem("q_hi_done"), [sem("spare_free0"), sem("spare_free1")]
        s_psum, abs_done, tri_done, max_done = sem("s_psum"), sem("abs_done"), sem("tri_done"), sem("max_done")
        maxT_psum, maxrow_psum = sem("maxT_psum"), sem("maxrow_psum")
        sub_done, exp_done, phi_done, plo_done = sem("sub_done"), sem("exp_done"), sem("phi_done"), sem("plo_done")
        pv_done, u_done, out_psum, rden_done = sem("pv_done"), sem("u_done"), sem("out_psum"), sem("rden_done")
        xr_in, xr_bo, x2_done, x2_stored = sem("xr_in"), sem("xr_bo"), sem("x2_done"), sem("x2_stored")

        block = ctx.enter_context(nc.Block())
        LOADS = 23
        POOL_CONSTS = NP + 9

        def wait_apart(eng, semaphore, value):
            eng.wait_ge(semaphore, value)
            eng.sem_inc(waited, 1)

        def barrier(eng, k):
            eng.drain().then_inc(phase_done, 1)
            wait_apart(eng, phase_done, 5 * k)

        def after_ffn(ph, b):
            return 2 + 3 * b if ph == 0 else 2 + 3 * B + b

        def seq(ph, b):
            return (ph * B + b) * NT

        BLOCKS = SUB * NT * (NT + 1) // 2

        def within(eng, value, largest):
            if isinstance(value, int):
                return value
            return eng.snap(nc.s_assert_within(value, 0, largest, skip_runtime_bounds_check_because="loop bounds"))

        def blocks(eng, b, j, m):
            return within(eng, b * BLOCKS + 2 * (j * (j + 1)) + SUB * m, B * BLOCKS)

        def ring_at(eng, j, m):
            if isinstance(j, int) and isinstance(m, int):
                return (j * (j + 1) // 2 + m) % RING * (SUB * TT)
            return within(eng, (((j * (j + 1)) >> 1) + m) % RING * (SUB * TT), (RING - 1) * SUB * TT)

        def spare(j):
            return 2 * NT - 1 if is_int(j, NT - 1) else 2 + 2 * j
        SPARE = 2 * NT

        def has_next(j, n):
            return not isinstance(j, int) or j + n < NT

        def has_o(j):
            return not isinstance(j, int) or j >= 1

        def is_int(j, value):
            return isinstance(j, int) and j == value

        def cols(a, at, n):
            return a[:, bass.ds(at, n)]

        def rows4(a):
            return a.rearrange("p (u d) -> p u d", u=SUB)

        def dram_tile(a, i):
            return a[bass.ds(i, 1)].rearrange("a p u d -> p (a u) d")

        def over_steps(eng, step):
            for j in range(3):
                step(j)
            with eng.Fori(3, NT - 2) as j:
                step(j)
            step(NT - 2)
            step(NT - 1)

        def over_pairs(eng, j, pair):
            if isinstance(j, int) and j < 2:
                return
            pair(0)
            if not is_int(j, 2):
                with eng.Fori(1, j - 1) as m:
                    pair(m)

        def over_turns(eng, turn):
            turn(-1)
            turn(0)
            with eng.Fori(1, NT - 2) as t:
                turn(t)
            turn(NT - 2)
            turn(NT - 1)

        def is_tile(t):
            return not isinstance(t, int) or 0 <= t < NT

        @block.sync
        def _(sp):
            def load(dst, src, columns=False):
                sp.dma_start(dst, src, allow_slow_non_contiguous=columns).then_inc(weights_in, 16)

            for i, w in enumerate((Wq, Wk, Wv)):
                load(wqkv_s[:, i * DC * D:(i + 1) * DC * D].rearrange("p (c d) -> p c d", c=DC),
                     w.rearrange("(c p) d -> p c d", p=P))
            for i, bias in enumerate((bq, bk, bv)):
                load(bqkv_s[:, DC * i:DC * i + DC], bias.rearrange("(c p) -> p c", p=P), columns=True)
            load(wo_s.rearrange("p (c d) -> p c d", c=DC), Wo.rearrange("(c p) d -> p c d", p=P))
            w1_v = w1_s.rearrange("p (c q m) -> p c q m", c=DC, m=DM)
            load(w1_v[:, :, 0, :], Wo1.rearrange("(c p) m -> p c m", p=P))
            for c in range(DC):
                load(w1_v[:, c, 1:, :], W1[:, c * P:(c + 1) * P, :].rearrange("e p m -> p e m"))
            b1_f = b1.rearrange("e m -> (e m)")
            load(b1_s[DM:P, 0:1], b1_f[0:DM].rearrange("(p a) -> p a", a=1))
            load(b1_s[:, 1:HC], b1_f[DM:].rearrange("(c p) -> p c", p=P), columns=True)
            load(bo1c[:, :], bo1.rearrange("(p a) -> p a", a=1))
            load(wo2[0:DM, :], Wo2)
            load(wo2[DM:DM + 1, :], bo2.rearrange("(a e) -> a e", a=1))
            for c in range(DC):
                load(kmix[:, c, :], mix[:, c * P:(c + 1) * P].rearrange("j p -> p j"), columns=True)
            load(gamma_b[:, :], gamma.partition_broadcast(P))
            load(beta_b[:, :], beta.partition_broadcast(P))
            load(bo_b[:, :], bo.partition_broadcast(P))
            w2_f = W2.rearrange("e m d -> (e m) d")
            w2_v = w2_s.rearrange("p (c d) -> p c d", c=HC)
            sp.wait_ge(w2_cleared, 1)
            load(w2_v[0:NP, 0, :], b2)
            load(w2_v[DM:P, 0, :], w2_f[0:DM, :])
            load(w2_v[:, 1:, :], w2_f[DM:, :].rearrange("(c p) d -> p c d", p=P))
            barrier(sp, 1)

            def ffn(ph, b, src, dst):
                g0 = seq(ph, b)
                for i in range(NT):
                    if i >= 4:
                        sp.wait_ge(x_in[i % 4], 4 * g0 + 16)
                    sp.dma_start(rows4(cols(X, i * SUB * D, SUB * D)), dram_tile(src, b * NT + i))\
                        .then_inc(x_in[i % 4], 16)
                with sp.Fori(0, NT) as t:
                    sp.wait_ge(x1_done, g0 + t + 2)
                    sp.dma_start(dram_tile(dst, b * NT + t), rows4(cols(N, t * SUB * D, SUB * D)))\
                        .then_inc(stored, 16)
                wait_apart(sp, stored, 16 * g0 + 16 * NT)

            def attention(b):
                with sp.Fori(0, NT) as j:
                    s = b * NT + j
                    sp.wait_ge(x2_stored, 16 * s + 1)
                    sp.dma_start(rows4(xr), dram_tile(x1_t, s)).then_inc(xr_in, 16)
                    sp.wait_ge(x2_done, SUB * s + SUB)
                    sp.dma_start(dram_tile(x2_t, s), rows4(xr)).then_inc(x2_stored, 16)
                wait_apart(sp, x2_stored, 16 * NT * b + 16 * NT + 1)

            sp.sem_inc(x2_stored, 1)
            with sp.Fori(0, B) as b:
                ffn(0, b, x_t, x1_t)
                barrier(sp, after_ffn(0, b))
                barrier(sp, after_ffn(0, b) + 1)
                attention(b)
                barrier(sp, after_ffn(0, b) + 2)
            with sp.Fori(0, B) as b:
                ffn(1, b, x2_t, out_t)
                barrier(sp, after_ffn(1, b))

        @block.gpsimd
        def _(pool):
            g = nc.gpsimd
            g.memset(th[DM:DM + 1, :], 1.0).then_inc(pool_const, 1)
            pool.wait_ge(pool_const, 1)
            g.memset(ident[:, :], 0.0).then_inc(pool_const, 1)
            g.memset(tri[:, :], 0.0).then_inc(pool_const, 1)
            g.memset(expand[:, :, :], 1.0).then_inc(pool_const, 1)
            g.memset(half[:, :], -0.5).then_inc(pool_const, 1)
            for e in range(NP):
                g.memset(prio[:, :, e:e + 1], float(NP - e)).then_inc(pool_const, 1)
            pool.wait_ge(pool_const, NP + 5)
            g.affine_select(out=ident[:, :], in_=ident[:, :], compare_op=ALU.not_equal, fill=1.0,
                            base=0, pattern=[[-1, P]], channel_multiplier=1).then_inc(pool_const, 1)
            g.affine_select(out=tri[:, :], in_=tri[:, :], compare_op=ALU.is_ge, fill=MASKED,
                            base=0, pattern=[[1, P]], channel_multiplier=-1).then_inc(pool_const, 1)
            expand_v = expand[:, :, :].rearrange("e c (k m) -> e (c k) m", m=DM)
            g.affine_select(out=expand_v, in_=expand_v, compare_op=ALU.is_equal, fill=0.0, base=-1,
                            pattern=[[1, 2 * HC], [0, DM]], channel_multiplier=-1).then_inc(pool_const, 1)
            pool.wait_ge(pool_const, NP + 8)
            g.affine_select(out=expand[:, 0, 0:DM], in_=expand[:, 0, 0:DM], compare_op=ALU.not_equal, fill=1.0,
                            base=0, pattern=[[-1, DM]], channel_multiplier=1).then_inc(pool_const, 1)
            barrier(pool, 1)

            def inverse_root(var_ready, eps_done, rstd_done, i, value, scale=1.0):
                wait_apart(pool, var_ready, value)
                g.tensor_scalar(veps[:, i, :], mv[:, i, :, 1], scale ** -2, EPS * scale ** -2, ALU.mult, ALU.add)\
                    .then_inc(eps_done, 1)
                pool.wait_ge(eps_done, value)
                g.tensor_tensor(rstd[:, i, :], veps[:, i, :], half[:, :], ALU.pow).then_inc(rstd_done, 1)

            def ffn(ph, b):
                g0 = seq(ph, b)
                with pool.Fori(0, NT // 2) as r:
                    for i in range(2):
                        inverse_root(n_var, n_eps, n_rstd, i, g0 + 2 * r + i + 1)
                with pool.Fori(0, NT) as t:
                    g_tile = g0 + t
                    pool.wait_ge(x1_done, g_tile + 1)
                    g.tensor_tensor(rows4(xb), rows4(cols(X, t * SUB * D, SUB * D)),
                                    beta_b[:, :].unsqueeze(1).to_broadcast([P, SUB, D]), ALU.add)\
                        .then_inc(xb_done, 1)
                    inverse_root(r_var, r_eps, r_rstd, 0, g_tile + 1)
                    g.tensor_scalar(r_neg[:, :], mv[:, 0, :, 0], -1.0, None, ALU.mult).then_inc(r_neg_done, 1)
                    wait_apart(pool, r_neg_done, g_tile + 1)
                    pool.wait_ge(r_rstd, g_tile + 1)
                    g.tensor_tensor(r_bias[:, :], r_neg[:, :], rstd[:, 0, :], ALU.mult).then_inc(r_bias_done, 1)
                    pool.wait_ge(z_done, g_tile + 1)
                    g.tensor_tensor(rows4(z), rows4(z), gamma_b[:, :].unsqueeze(1).to_broadcast([P, SUB, D]),
                                    ALU.mult).then_inc(r_mid, 1)
                    pool.wait_ge(r_mid, g_tile + 1)
                    pool.wait_ge(xb_done, g_tile + 1)
                    g.tensor_tensor(cols(N, t * SUB * D, SUB * D), z, xb, ALU.add).then_inc(x1_done, 1)

            def attention_input(b):
                with pool.Fori(0, NT) as t:
                    inverse_root(a_var, a_eps, a_rstd, 0, b * NT + t + 1, scale=XS)

            def attention(b):
                with pool.Fori(0, NT) as j:
                    s = b * NT + j
                    pool.wait_ge(xr_in, 16 * s + 16)
                    g.tensor_tensor(rows4(xr), rows4(xr), bo_b[:, :].unsqueeze(1).to_broadcast([P, SUB, D]),
                                    ALU.add).then_inc(xr_bo, 1)

            with pool.Fori(0, B) as b:
                ffn(0, b)
                barrier(pool, after_ffn(0, b))
                attention_input(b)
                barrier(pool, after_ffn(0, b) + 1)
                attention(b)
                barrier(pool, after_ffn(0, b) + 2)
            with pool.Fori(0, B) as b:
                ffn(1, b)
                barrier(pool, after_ffn(1, b))

        @block.vector
        def _(dve):
            v = nc.vector
            v.memset(w2_s[:, 0:D], 0.0).then_inc(w2_cleared, 1)
            dve.wait_ge(weights_in, 16 * LOADS)
            v.tensor_reduce(off_s[:, 0:3 * DC], wqkv_s.rearrange("p (i d) -> p i d", d=D), AX.X, ALU.add)
            v.tensor_scalar(bqkv_s[:, 0:3 * DC], bqkv_s[:, 0:3 * DC], 1.0 / (D * BETA), None, ALU.mult)\
                .then_inc(fold_step, 1)
            dve.wait_ge(fold_step, 1)
            v.scalar_tensor_tensor(out=off_s[:, 0:3 * DC], in0=off_s[:, 0:3 * DC], scalar=-1.0 / D,
                                   in1=bqkv_s[:, 0:3 * DC], op0=ALU.mult, op1=ALU.add).then_inc(fold_step, 1)
            dve.wait_ge(fold_step, 2)
            for i in range(3 * DC):
                v.tensor_scalar(cols(wqkv_s, i * D, D), cols(wqkv_s, i * D, D), off_s[:, i:i + 1], None, ALU.add)\
                    .then_inc(folded, 1)
            w1h, w1l, w2h, w2l = (a[:, :, :].rearrange("p a b -> p (a b)") for a in (w1_hi, w1_lo, w2_hi, w2_lo))
            v.tensor_scalar(w1h, w1_s, WS, None, ALU.mult)
            v.tensor_scalar(w2h, w2_s, WS, None, ALU.mult).then_inc(fold_step, 1)
            dve.wait_ge(fold_step, 3)
            v.scalar_tensor_tensor(out=w1l, in0=w1_s, scalar=WS, in1=w1h, op0=ALU.mult, op1=ALU.subtract)
            v.scalar_tensor_tensor(out=w2l, in0=w2_s, scalar=WS, in1=w2h, op0=ALU.mult, op1=ALU.subtract)
            v.tensor_scalar(b1c[:, 1:HC], b1_s[:, 1:HC], XS, None, ALU.mult)
            v.tensor_scalar(b1c[DM:P, 0:1], b1_s[DM:P, 0:1], XS, None, ALU.mult)
            v.tensor_scalar(kmix[:, :, :], kmix[:, :, :], XS, None, ALU.mult)
            v.tensor_scalar(gamma_b[:, :], gamma_b[:, :], 0.5, None, ALU.mult)
            v.tensor_scalar(beta_b[:, :], beta_b[:, :], 0.5, None, ALU.mult)
            v.memset(wvo[:, :, D:D + 8], 1.0 / (D * BETA))
            dve.wait_ge(pool_const, POOL_CONSTS)
            v.tensor_copy(ident16[:, :], ident[:, :])
            dve.wait_ge(woT_psum, 1)
            v.tensor_copy(wo_t, PS[:, 2, :]).then_inc(woT_done, 1)
            dve.wait_ge(wqk_psum, 1)
            for c in range(DC):
                v.tensor_scalar(wqk_hi[:, c, :], PS[:, c, 0:D], WS, None, ALU.mult).then_inc(fold_step, 1)
            dve.wait_ge(fold_step, 3 + DC)
            for c in range(DC):
                v.scalar_tensor_tensor(out=wqk_lo[:, c, :], in0=PS[:, c, 0:D], scalar=WS, in1=wqk_hi[:, c, :],
                                       op0=ALU.mult, op1=ALU.subtract)
            dve.wait_ge(wvo_psum, 1)
            for c in range(DC):
                v.tensor_copy(wvo[:, c, 0:D], PS[:, 3 + c, 0:D])
            dve.sem_inc(x1_done, 1)
            dve.sem_inc(y_done, 2)
            dve.sem_inc(hm_done, 2)
            dve.sem_inc(aT_lo, DC)
            dve.sem_inc(plo_done, 2)
            dve.sem_inc(spare_free[0], 1)
            dve.sem_inc(spare_free[1], 1)
            barrier(dve, 1)

            def row_stats(src, at, i, stat_done, var_done, value):
                for u in range(SUB):
                    ins = v.bn_stats(st[:, i, u, :], cols(src, at + u * D, D))
                ins.then_inc(stat_done, 1)
                wait_apart(dve, stat_done, value)
                for u in range(SUB):
                    ins = v.bn_aggr(mv[:, i, u, :], st[:, i, u, :])
                ins.then_inc(var_done, 1)

            def ffn(ph, b):
                g0 = seq(ph, b)
                nT_v = nT.rearrange("p (c s) -> p c s", c=DC)
                v.memset(nT_v[:, :, 0:1], 0.0)
                v.memset(nT_v[:, :, S + 1:S + 2], 0.0)
                v.memset(hb[0:DM, 0:TT], XS).then_inc(edges_set, 1)

                def normalise(t, i):
                    dve.wait_ge(n_rstd, g0 + t + 1)
                    dve.wait_ge(n_kept, g0 + t + 1)
                    for u in range(SUB):
                        ins = v.tensor_scalar(cols(Ns, (i % 2) * SUB * D + u * D, D), cols(X, t * SUB * D + u * D, D),
                                              mv[:, i % 2, u, 0:1], rstd[:, i % 2, u:u + 1], ALU.subtract, ALU.mult)
                    ins.then_inc(n_done, 1)

                with dve.Fori(0, NT // 4) as r:
                    for i in range(4):
                        t = 4 * r + i
                        dve.wait_ge(x_in[i], 4 * g0 + 16 * r + 16)
                        row_stats(X, t * SUB * D, i % 2, n_stat, n_var, g0 + t + 1)
                        if i >= 1:
                            normalise(t - 1, i - 1)
                    normalise(4 * r + 3, 3)
                dve.wait_ge(nT_done, DC * (g0 + NT) + DC)
                dve.wait_ge(edges_set, (ph * B + b) + 1)

                def mixed(t, c):
                    k = DC * (g0 + t)
                    xm_c, at = cols(xm, c * TT, TT), c * NTC + t * TT
                    dve.wait_ge(xa_done, k + c + 1)
                    v.scalar_tensor_tensor(out=xm_c, in0=cols(nT, at, TT), scalar=kmix[:, c, 0:1],
                                           in1=cols(xa, c * TT, TT), op0=ALU.mult, op1=ALU.add).then_inc(mix_part, 1)
                    dve.wait_ge(mix_part, k + c + 1)
                    v.scalar_tensor_tensor(out=xm_c, in0=cols(nT, at + 2, TT), scalar=kmix[:, c, 2:3],
                                           in1=xm_c, op0=ALU.mult, op1=ALU.add).then_inc(mix_done, 1)

                def mixed_low(t):
                    for c in range(DC):
                        dve.wait_ge(xhi_done, DC * (g0 + t) + c + 1)
                        at = (t & 1) * (DC * TT) + c * TT
                        v.tensor_tensor(cols(xlo, at, TT), cols(xm, c * TT, TT), cols(xhi, at, TT),
                                        ALU.subtract).then_inc(xlo_done, 1)

                def result(t):
                    dve.wait_ge(o_psum, g0 + t + 1)
                    if not is_int(t, 0):
                        dve.wait_ge(z_done, g0 + t)
                    for i in range(2):
                        v.scalar_tensor_tensor(out=cols(y, i * TT, TT), in0=ps_o[:, i, :], scalar=1.0 / (XS * WS),
                                               in1=cols(N, t * SUB * D + i * TT, TT), op0=ALU.mult, op1=ALU.add)\
                            .then_inc(y_done, 1)

                def result_stats(t):
                    dve.wait_ge(y_done, 2 * (g0 + t) + 4)
                    row_stats(y, 0, 0, r_stat, r_var, g0 + t + 1)

                def route(t):
                    k = 4 * (g0 + t)
                    dve.wait_ge(route_psum, g0 + t + 1)
                    v.tensor_reduce(r_max[:, :], ps_route, AX.X, ALU.max).then_inc(route_step, 1)
                    dve.wait_ge(route_step, k + 1)
                    v.tensor_tensor(r_eq[:, :, :], ps_route, r_max[:, :].unsqueeze(2).to_broadcast([P, SUB, NP]),
                                    ALU.is_equal).then_inc(route_step, 1)
                    dve.wait_ge(route_step, k + 2)
                    v.tensor_tensor(r_pr[:, :, :], r_eq[:, :, :], prio[:, :, :], ALU.mult).then_inc(route_step, 1)
                    dve.wait_ge(route_step, k + 3)
                    v.tensor_reduce(r_top[:, :], r_pr[:, :, :], AX.X, ALU.max).then_inc(route_step, 1)
                    dve.wait_ge(route_step, k + 4)
                    v.tensor_tensor(oh[:, :, :], r_pr[:, :, :], r_top[:, :].unsqueeze(2).to_broadcast([P, SUB, NP]),
                                    ALU.is_equal).then_inc(oh_done, 1)

                def masked(t, c):
                    k = HC * (g0 + t) + c
                    dve.wait_ge(hb_done, k + 3)
                    if c >= 2 or not is_int(t, 0):
                        dve.wait_ge(hlo_done, k if c == 0 else k - 1)
                    dve.wait_ge(mask_psum, k + 1)
                    v.tensor_tensor(cols(hm, (c % 2) * TT, TT), ps_m[:, c % 2, :], cols(hb, c * TT, TT), ALU.mult)\
                        .then_inc(hm_done, 1)

                def masked_low(t, c):
                    dve.wait_ge(hhi_done, HC * (g0 + t) + c + 1)
                    v.tensor_tensor(cols(hlo, c * TT, TT), cols(hm, (c % 2) * TT, TT), cols(hhi, c * TT, TT),
                                    ALU.subtract).then_inc(hlo_done, 1)

                def turn(t):
                    second, choice, mix, normal = is_tile(t), is_tile(t + 1), is_tile(t + 2), is_tile(t - 1)
                    if normal:
                        result(t - 1)
                    if second:
                        masked(t, 2)
                        masked_low(t, 1)
                    if normal:
                        result_stats(t - 1)
                    if second:
                        masked(t, 3)
                        masked_low(t, 2)
                    if choice:
                        route(t + 1)
                    if mix:
                        mixed(t + 2, 0)
                    if second:
                        masked(t, 4)
                        masked_low(t, 3)
                    if mix:
                        mixed(t + 2, 1)
                    if second:
                        masked_low(t, 4)
                    if mix:
                        mixed_low(t + 2)
                    if choice:
                        masked(t + 1, 0)
                        masked(t + 1, 1)
                        masked_low(t + 1, 0)

                for c in range(DC):
                    mixed(0, c)
                mixed_low(0)
                over_turns(dve, turn)
                result(NT - 1)
                result_stats(NT - 1)

            def attention_input(b):
                def normalise(t):
                    dve.wait_ge(a_rstd, b * NT + t + 1)
                    for u in range(SUB):
                        ins = v.tensor_scalar(cols(Ns, (t & 1) * SUB * D + u * D, D), cols(N, t * SUB * D + u * D, D), mv[:, 0, u, 0:1], rstd[:, 0, u:u + 1],
                                              ALU.subtract, ALU.mult)
                    ins.then_inc(a_done, 1)

                def stats(t):
                    row_stats(N, t * SUB * D, 0, a_stat, a_var, b * NT + t + 1)

                def lows(t):
                    dve.wait_ge(a_hi, b * NT + t + 1)
                    v.scalar_tensor_tensor(out=cols(KV_lo, t * SUB * D, SUB * D), in0=cols(Ns, (t & 1) * SUB * D, SUB * D),
                                           scalar=XS * BETA, in1=cols(KV_hi, t * SUB * D, SUB * D),
                                           op0=ALU.add, op1=ALU.subtract)
                    for c in range(DC):
                        dve.wait_ge(aT_hi, DC * (b * NT + t) + c + 1)
                        v.scalar_tensor_tensor(out=cols(KT_lo, c * S + t * TT, TT), in0=ps_o[:, c, :],
                                               scalar=XS * BETA, in1=cols(KT_hi, c * S + t * TT, TT),
                                               op0=ALU.add, op1=ALU.subtract).then_inc(aT_lo, 1)

                for t in range(2):
                    stats(t)
                    normalise(t)
                with dve.Fori(0, NT - 2) as t:
                    stats(t + 2)
                    lows(t)
                    dve.wait_ge(aT_lo, DC * (b * NT + t) + 2 * DC)
                    normalise(t + 2)
                lows(NT - 2)
                lows(NT - 1)

            def attention(b):
                def q_low(j, c):
                    dve.wait_ge(q_hi_done, DC * (b * NT + j) + c + 1)
                    at = (j & 1) * (DC * TT) + c * TT
                    v.scalar_tensor_tensor(out=cols(q_lo, at, TT), in0=ps_x[:, c, :], scalar=QS / (XS * WS),
                                           in1=cols(q_hi, at, TT), op0=ALU.mult, op1=ALU.subtract)\
                        .then_inc(spare_free[c], 1)

                def score_max(j, m, i, diagonal, before, ring_m):
                    n = before + i
                    lo = i * P if diagonal else 0
                    at = ring_m + i * TT + lo
                    dve.wait_ge(abs_done, n + SUB + 1)
                    if diagonal:
                        v.tensor_tensor(cols(ring, at, P), cols(ring, at, P), tri[:, :], ALU.add)\
                            .then_inc(tri_done, 1)
                        dve.wait_ge(tri_done, SUB * (b * NT + j) + i + 1)
                    if isinstance(m, int) and m == 0 and i == 0:
                        v.tensor_copy(run_max[:, :], cols(ring, at, TT)).then_inc(max_done, 1)
                    else:
                        dve.wait_ge(max_done, n)
                        v.tensor_tensor(run_max[:, lo:], run_max[:, lo:], cols(ring, at, TT - lo), ALU.max)\
                            .then_inc(max_done, 1)

                def shifted(i, diagonal, ring_n):
                    lo = i * P if diagonal else 0
                    at = ring_n + i * TT + lo
                    v.tensor_tensor(cols(ring, at, TT - lo), cols(ring, at, TT - lo), max_row[:, lo:], ALU.subtract)\
                        .then_inc(sub_done, 1)

                def p_low(i, diagonal, before):
                    lo = i * P if diagonal else 0
                    dve.wait_ge(phi_done, before + i + 1)
                    v.tensor_tensor(p_lo[:, i * TT + lo:(i + 1) * TT], pf[:, (i % 2) * TT + lo:(i % 2 + 1) * TT],
                                    p_hi[:, i * TT + lo:(i + 1) * TT], ALU.subtract).then_inc(plo_done, 1)

                def output(s, u):
                    if u == 0:
                        dve.wait_ge(xr_bo, s + 1)
                    dve.wait_ge(out_psum, SUB * s + u + 1)
                    v.reciprocal(rden[:, u:u + 1], ps_x[:, u % 2, D:D + 1]).then_inc(rden_done, 1)
                    dve.wait_ge(rden_done, SUB * s + u + 1)
                    v.scalar_tensor_tensor(out=cols(xr, u * D, D), in0=ps_x[:, u % 2, 0:D],
                                           scalar=rden[:, u:u + 1], in1=cols(xr, u * D, D),
                                           op0=ALU.mult, op1=ALU.add).then_inc(x2_done, 1)

                def group(score, value, beside):
                    if score:
                        s_before, s_ring = blocks(dve, b, *score[:2]), ring_at(dve, *score[:2])
                    if value:
                        v_before, v_ring = blocks(dve, b, *value[:2]), ring_at(dve, *value[:2])
                    for i in range(SUB):
                        if value:
                            if i == 0 and is_int(value[1], 0):
                                dve.wait_ge(spare_free[1], b * SPARE + spare(value[0]) + 2)
                            shifted(i, value[2], v_ring)
                            if i >= 1:
                                p_low(i - 1, value[2], v_before)
                            elif not is_int(value[1], 0):
                                p_low(SUB - 1, False, v_before - SUB)
                        if score:
                            score_max(score[0], score[1], i, score[2], s_before, s_ring)
                        beside(i)
                    if value and value[2]:
                        p_low(SUB - 1, True, v_before)
                    beside(SUB)

                def step(j):
                    s = b * NT + j
                    dve.wait_ge(maxT_psum, s + 1)
                    v.tensor_reduce(max_col[:, :], rows4(ps_x[:, 0, :]), AX.X, ALU.max).then_inc(spare_free[0], 1)

                    def first(i):
                        if is_int(j, 0) and i == SUB:
                            for c in range(DC):
                                q_low(j + 2, c)

                    def last_pair(i):
                        if has_next(j, 2):
                            if is_int(j, 1) and i in (2, 3):
                                q_low(j + 2, i - 2)
                            if not is_int(j, 1) and i < DC:
                                q_low(j + 2, i)

                    def diagonal(i):
                        if has_o(j) and i != 2:
                            output(s - 1, {0: 0, 1: 1, 3: 2, SUB: 3}[i])

                    more = has_next(j, 1)
                    if more:
                        group((j + 1, 0, False), None, first)
                    over_pairs(dve, j, lambda m: group((j + 1, m + 1, False) if more else None, (j, m, False),
                                                       lambda i: None))
                    if has_o(j):
                        group((j + 1, j, False) if more else None, (j, j - 1, False), last_pair)
                    group((j + 1, j + 1, True) if more else None, (j, j, True), diagonal)

                for j in range(2):
                    for c in range(DC):
                        q_low(j, c)
                group((0, 0, True), None, lambda i: None)
                over_steps(dve, step)
                for u in range(SUB):
                    output(b * NT + NT - 1, u)

            with dve.Fori(0, B) as b:
                ffn(0, b)
                barrier(dve, after_ffn(0, b))
                attention_input(b)
                barrier(dve, after_ffn(0, b) + 1)
                attention(b)
                barrier(dve, after_ffn(0, b) + 2)
            with dve.Fori(0, B) as b:
                ffn(1, b)
                barrier(dve, after_ffn(1, b))

        @block.scalar
        def _(act):
            a = nc.scalar
            act.sem_inc(nT_done, DC)
            act.sem_inc(n_kept, 2)
            act.sem_inc(hb_done, 2)
            act.sem_inc(abs_done, SUB)
            act.sem_inc(u_done, 1)
            barrier(act, 1)

            def ffn(ph, b):
                g0 = seq(ph, b)
                with act.Fori(0, NT) as t:
                    for c in range(DC):
                        act.wait_ge(nT_psum, DC * (g0 + t) + c + 1)
                        a.activation(cols(nT, c * NTC + t * TT + 1, TT), ps_o[:, c, :], ACT.Copy).then_inc(nT_done, 1)
                    act.wait_ge(n_done, g0 + t + 1)
                    a.activation(cols(N, t * SUB * D, SUB * D), cols(Ns, (t & 1) * SUB * D, SUB * D), ACT.Copy)\
                        .then_inc(n_kept, 1)
                act.wait_ge(nT_done, DC * (g0 + NT) + DC)

                def middle(t):
                    for c in range(DC):
                        if not is_int(t, 0):
                            act.wait_ge(mix_part, DC * (g0 + t))
                        a.activation(cols(xa, c * TT, TT), cols(nT, c * NTC + t * TT + 1, TT), ACT.Copy,
                                     scale=kmix[:, c, 1:2]).then_inc(xa_done, 1)

                def x_high(t):
                    for c in range(DC):
                        act.wait_ge(mix_done, DC * (g0 + t) + c + 1)
                        a.activation(cols(xhi, (t & 1) * (DC * TT) + c * TT, TT), cols(xm, c * TT, TT), ACT.Copy)\
                            .then_inc(xhi_done, 1)

                def hidden(t, c):
                    k = HC * (g0 + t) + c
                    act.wait_ge(h_psum, k + 1)
                    if c == 0:
                        a.activation(th[0:DM, :], ps_h[0:DM, 0, :], ACT.Tanh, bias=bo1c[:, :], scale=1.0 / (XS * WS))\
                            .then_inc(tanh_done, 1)
                    if not is_int(t, 0):
                        act.wait_ge(hm_done, k - HC + 3)
                    rows = slice(DM if c == 0 else 0, P)
                    a.activation(hb[rows, c * TT:(c + 1) * TT], ps_h[rows, c % 2, :], ACT.Identity,
                                 bias=b1c[rows, c:c + 1], scale=1.0 / WS).then_inc(hb_done, 1)

                def one_hot(t):
                    act.wait_ge(ohT_psum, g0 + t + 1)
                    a.activation(oh_t[:, :], ps_oh[0:NP, 0:TT], ACT.Copy).then_inc(ohT_done, 1)

                def masked_high(t, c):
                    act.wait_ge(hm_done, HC * (g0 + t) + c + 3)
                    a.activation(cols(hhi, c * TT, TT), cols(hm, (c % 2) * TT, TT), ACT.Copy).then_inc(hhi_done, 1)

                def normal(t):
                    act.wait_ge(x1_done, g0 + t + 1)
                    act.wait_ge(r_bias_done, g0 + t + 1)
                    for u in range(SUB):
                        ins = a.activation(cols(z, u * D, D), cols(y, u * D, D), ACT.Identity,
                                           bias=r_bias[:, u:u + 1], scale=rstd[:, 0, u:u + 1])
                    ins.then_inc(z_done, 1)

                def turn(t):
                    second, first, mix = is_tile(t), is_tile(t + 1), is_tile(t + 2)
                    if first:
                        hidden(t + 1, 0)
                        hidden(t + 1, 1)
                    if second:
                        masked_high(t, 2)
                    if mix:
                        middle(t + 2)
                    if second:
                        masked_high(t, 3)
                    if first:
                        hidden(t + 1, 2)
                    if is_tile(t - 1):
                        normal(t - 1)
                    if second:
                        masked_high(t, 4)
                    if first:
                        hidden(t + 1, 3)
                        one_hot(t + 1)
                    if mix:
                        x_high(t + 2)
                    if first:
                        hidden(t + 1, 4)
                        masked_high(t + 1, 0)
                        masked_high(t + 1, 1)

                middle(0)
                x_high(0)
                over_turns(act, turn)
                normal(NT - 1)

            def attention_input(b):
                with act.Fori(0, NT) as t:
                    g = b * NT + t
                    act.wait_ge(a_done, g + 1)
                    a.activation(cols(KV_hi, t * SUB * D, SUB * D), cols(Ns, (t & 1) * SUB * D, SUB * D), ACT.Copy,
                                 bias=XS * BETA).then_inc(a_hi, 1)
                    for c in range(DC):
                        act.wait_ge(aT_psum, DC * g + c + 1)
                        a.activation(cols(KT_hi, c * S + t * TT, TT), ps_o[:, c, :], ACT.Copy, bias=XS * BETA)\
                            .then_inc(aT_hi, 1)

            def attention(b):
                def q_high(j, c):
                    act.wait_ge(q_psum, DC * (b * NT + j) + c + 1)
                    a.activation(cols(q_hi, (j & 1) * (DC * TT) + c * TT, TT), ps_x[:, c, :], ACT.Copy,
                                 scale=QS / (XS * WS)).then_inc(q_hi_done, 1)

                def absolute(i, diagonal, before, ring_m):
                    lo = i * P if diagonal else 0
                    act.wait_ge(s_psum, before + i + 1)
                    a.activation(cols(ring, ring_m + i * TT + lo, TT - lo), ps_s[:, i, lo:], ACT.Abs,
                                 scale=1.0 / (QS * XS * D ** 0.5)).then_inc(abs_done, 1)

                def probability(i, diagonal, before, ring_n):
                    lo = i * P if diagonal else 0
                    k = before + i
                    p = pf[:, (i % 2) * TT + lo:(i % 2 + 1) * TT]
                    act.wait_ge(plo_done, k + 1)
                    act.wait_ge(sub_done, k + 1)
                    a.activation(p, cols(ring, ring_n + i * TT + lo, TT - lo), ACT.Exp)\
                        .then_inc(exp_done, 1)
                    act.wait_ge(pv_done, k + 1)
                    act.wait_ge(exp_done, k + 1)
                    a.activation(p_hi[:, i * TT + lo:(i + 1) * TT], p, ACT.Copy).then_inc(phi_done, 1)

                def weighted(j):
                    act.wait_ge(pv_done, blocks(act, b, j + 1, 0) + SUB)
                    if has_o(j):
                        act.wait_ge(out_psum, SUB * (b * NT + j))
                    a.activation(U[:, 0:TT], ps_u[:, 0, :], ACT.Copy)
                    a.activation(U[:, TT:], ps_u[:, 1, :], ACT.Copy).then_inc(u_done, 1)

                def group(before, score, value, beside):
                    if before:
                        p_before, p_ring = blocks(act, b, *before[:2]), ring_at(act, *before[:2])
                    if score:
                        s_before, s_ring = blocks(act, b, *score[:2]), ring_at(act, *score[:2])
                    if value:
                        v_before, v_ring = blocks(act, b, *value[:2]), ring_at(act, *value[:2])
                    for i in range(SUB):
                        if value:
                            probability(i, value[2], v_before, v_ring)
                        if before and i == 0:
                            absolute(SUB - 1, before[2], p_before, p_ring)
                        if score and i >= 1:
                            absolute(i - 1, score[2], s_before, s_ring)
                        beside(i)

                def step(j):
                    more, more2 = has_next(j, 1), has_next(j, 2)

                    def maxima():
                        act.wait_ge(maxrow_psum, b * NT + j + 1)
                        a.activation(max_row[:, :], ps_x[:, 1, :], ACT.Copy, bias=-P_LOG).then_inc(spare_free[1], 1)

                    def first(i):
                        if i == 2:
                            maxima()
                        if is_int(j, 0) and i >= 2:
                            q_high(j + 2, i - 2)

                    def last_pair(i):
                        if more2:
                            if is_int(j, 1) and i in (2, 3):
                                q_high(j + 2, i - 2)
                            if not is_int(j, 1) and i == 0:
                                for c in range(DC):
                                    q_high(j + 2, c)

                    if has_o(j):
                        weighted(j - 1)
                    if more:
                        group((j + 1, 0, False), (j + 1, 1, is_int(j, 0)), None, first)
                    else:
                        maxima()
                    over_pairs(act, j, lambda m: group((j + 1, m + 1, False) if more else None,
                                                       (j + 1, m + 2, False) if more else None,
                                                       (j, m, False), lambda i: None))
                    if has_o(j):
                        group((j + 1, j, False) if more else None, (j + 1, j + 1, True) if more else None,
                              (j, j - 1, False), last_pair)
                    group((j + 1, j + 1, True) if more else None, (j + 2, 0, False) if more2 else None,
                          (j, j, True), lambda i: None)

                for j in range(2):
                    for c in range(DC):
                        q_high(j, c)
                group(None, (0, 0, True), None, lambda i: None)
                group((0, 0, True), (1, 0, False), None, lambda i: None)
                over_steps(act, step)
                weighted(NT - 1)

            with act.Fori(0, B) as b:
                ffn(0, b)
                barrier(act, after_ffn(0, b))
                attention_input(b)
                barrier(act, after_ffn(0, b) + 1)
                attention(b)
                barrier(act, after_ffn(0, b) + 2)
            with act.Fori(0, B) as b:
                ffn(1, b)
                barrier(act, after_ffn(1, b))

        @block.tensor
        def _(pe):
            t_ = nc.tensor

            def split_product(dst, pairs, start, stop, skip=False):
                last = 3 * len(pairs) - 1
                n = 0
                for (w_h, w_l), (x_h, x_l) in pairs:
                    for w, xx in ((w_h, x_h), (w_h, x_l), (w_l, x_h)):
                        ins = t_.matmul(dst, w, xx, start=start and n == 0, stop=stop and n == last,
                                        skip_group_check=skip)
                        n += 1
                return ins

            def transpose_rows(i, c):
                for u in range(SUB):
                    ins = t_.transpose(ps_o[:, c, u * P:(u + 1) * P], cols(Ns, (i * SUB + u) * D + c * P, P), ident[:, :])
                return ins

            pe.sem_inc(pv_done, SUB)
            pe.wait_ge(weights_in, 16 * LOADS)
            pe.wait_ge(pool_const, POOL_CONSTS)
            for c in range(DC):
                for d in range(DC):
                    ins = t_.transpose(PS[:, 2, d * D + c * P:d * D + (c + 1) * P],
                                       wo_s[:, c * D + d * P:c * D + (d + 1) * P], ident[:, :])
            ins.then_inc(woT_psum, 1)
            pe.wait_ge(folded, 3 * DC)
            wq_f, wk_f, wv_f = (wqkv_s[:, i * DC * D:(i + 1) * DC * D] for i in range(3))
            for d in range(DC):
                for c in range(DC):
                    ins = t_.matmul(PS[:, d, 0:D], wq_f[:, c * D + d * P:c * D + (d + 1) * P],
                                    wk_f[:, c * D:(c + 1) * D], start=c == 0, stop=c == DC - 1)
            ins.then_inc(wqk_psum, 1)
            pe.wait_ge(woT_done, 1)
            for d in range(DC):
                for c in range(DC):
                    ins = t_.matmul(PS[:, 3 + d, 0:D], wv_f[:, c * D + d * P:c * D + (d + 1) * P],
                                    wo_t[:, c * D:(c + 1) * D], start=c == 0, stop=c == DC - 1)
            ins.then_inc(wvo_psum, 1)
            barrier(pe, 1)

            def ffn(ph, b):
                g0 = seq(ph, b)
                with pe.Fori(0, NT // 2) as r:
                    for i in range(2):
                        g = g0 + 2 * r + i
                        pe.wait_ge(n_done, g + 1)
                        for c in range(DC):
                            pe.wait_ge(nT_done, DC * g + c + 1)
                            transpose_rows(i, c).then_inc(nT_psum, 1)

                def hidden(t, c):
                    k = HC * (g0 + t)
                    pe.wait_ge(hb_done, k + (2, 1, 3, 4, 5)[c])
                    x_at = (t & 1) * (DC * TT)
                    split_product(ps_h[:, c % 2, :],
                                  [((w1_hi[:, d, c * P:(c + 1) * P], w1_lo[:, d, c * P:(c + 1) * P]),
                                    (cols(xhi, x_at + d * TT, TT), cols(xlo, x_at + d * TT, TT)))
                                   for d in range(DC)], True, True).then_inc(h_psum, 1)

                def route(t):
                    pe.wait_ge(tanh_done, g0 + t + 1)
                    for u in range(SUB):
                        ins = t_.matmul(ps_route[:, u, :], th[:, u * P:(u + 1) * P], wo2[:, :], start=True, stop=True)
                    ins.then_inc(route_psum, 1)

                def choice(t):
                    pe.wait_ge(oh_done, g0 + t + 1)
                    for u in range(SUB):
                        ins = t_.transpose(ps_oh[0:NP, u * P:(u + 1) * P], oh[:, u, :], ident16[:, :])
                    ins.then_inc(ohT_psum, 1)

                def mask(t, c):
                    k = HC * (g0 + t)
                    if c == 0:
                        pe.wait_ge(ohT_done, g0 + t + 1)
                    pe.wait_ge(hm_done, k + (2, 2, 3, 4, 5)[c])
                    t_.matmul(ps_m[:, c % 2, :], expand[:, c, :], oh_t[:, :], start=True, stop=True)\
                        .then_inc(mask_psum, 1)

                def path(t, c):
                    if c == 0:
                        pe.wait_ge(y_done, 2 * (g0 + t) + 2)
                    pe.wait_ge(hlo_done, HC * (g0 + t) + c + 1)
                    for u in range(SUB):
                        at = c * TT + u * P
                        ins = split_product(ps_o[:, u // 2, (u % 2) * D:(u % 2 + 1) * D],
                                            [((cols(hhi, at, P), cols(hlo, at, P)), (w2_hi[:, c, :], w2_lo[:, c, :]))],
                                            c == 0 and u % 2 == 0, c == HC - 1, skip=True)
                    if c == HC - 1:
                        ins.then_inc(o_psum, 1)

                def turn(t):
                    second, first = is_tile(t), is_tile(t + 1)
                    if first:
                        pe.wait_ge(xlo_done, DC * (g0 + t + 1) + DC)
                        hidden(t + 1, 0)
                    if second:
                        mask(t, 2)
                    if first:
                        hidden(t + 1, 1)
                    if second:
                        path(t, 0)
                        mask(t, 3)
                    if first:
                        route(t + 1)
                        hidden(t + 1, 2)
                    if second:
                        path(t, 1)
                        mask(t, 4)
                    if first:
                        hidden(t + 1, 3)
                    if second:
                        path(t, 2)
                    if first:
                        choice(t + 1)
                        hidden(t + 1, 4)
                    if second:
                        path(t, 3)
                    if first:
                        mask(t + 1, 0)
                        mask(t + 1, 1)
                    if second:
                        path(t, 4)

                over_turns(pe, turn)

            def attention_input(b):
                with pe.Fori(0, NT // 2) as r:
                    for i in range(2):
                        g = b * NT + 2 * r + i
                        pe.wait_ge(a_done, g + 1)
                        for c in range(DC):
                            pe.wait_ge(aT_lo, DC * g + c + 1)
                            transpose_rows(i, c).then_inc(aT_psum, 1)

            def attention(b):
                def query(j, k, c):
                    pe.wait_ge(spare_free[c], k + 1)
                    split_product(ps_x[:, c, :],
                                  [((wqk_hi[:, d, c * P:(c + 1) * P], wqk_lo[:, d, c * P:(c + 1) * P]),
                                    (cols(KT_hi, d * S + j * TT, TT), cols(KT_lo, d * S + j * TT, TT)))
                                   for d in range(DC)], True, True).then_inc(q_psum, 1)

                def scores(before, m, i, q, diagonal):
                    lo = i * P if diagonal else 0
                    pe.wait_ge(abs_done, before + i + 1)
                    at = m * TT + i * P
                    split_product(ps_s[:, i, lo:],
                                  [((cols(KT_hi, d * S + at, P), cols(KT_lo, d * S + at, P)),
                                    (cols(q_hi, q + lo + d * TT, TT - lo), cols(q_lo, q + lo + d * TT, TT - lo)))
                                   for d in range(DC)], True, True).then_inc(s_psum, 1)

                def values(before, m, i, diagonal):
                    lo = i * P if diagonal else 0
                    pe.wait_ge(plo_done, before + i + 3)
                    at = (m * SUB + i) * D
                    for c in range(DC):
                        ins = split_product(ps_u[:, c, lo:],
                                            [((cols(KV_hi, at + c * P, P), cols(KV_lo, at + c * P, P)),
                                              (p_hi[:, i * TT + lo:(i + 1) * TT], p_lo[:, i * TT + lo:(i + 1) * TT]))],
                                            is_int(m, 0) and i == 0, i == SUB - 1, skip=True)
                    ins.then_inc(pv_done, 1)

                def output(s, k, u):
                    if u == 0:
                        pe.wait_ge(u_done, s + 2)
                    if u < 2:
                        pe.wait_ge(spare_free[u], k + 1)
                    else:
                        pe.wait_ge(x2_done, SUB * s + u - 1)
                    for c in range(DC):
                        ins = t_.matmul(ps_x[:, u % 2, 0:D + 1], U[:, c * TT + u * P:c * TT + (u + 1) * P],
                                        wvo[:, c, 0:D + 1], start=c == 0, stop=c == DC - 1)
                    ins.then_inc(out_psum, 1)

                def group(score, value, beside):
                    if score:
                        s_before, q = blocks(pe, b, *score[:2]), (score[0] & 1) * (DC * TT)
                    if value:
                        v_before = blocks(pe, b, *value[:2])
                    if score and is_int(score[1], 0):
                        uses = 0 if is_int(score[0], 0) else 2 * score[0] - 1
                        for c in range(DC):
                            pe.wait_ge(spare_free[c], b * SPARE + uses + 2)
                    for i in range(SUB):
                        if score:
                            scores(s_before, score[1], i, q, score[2])
                        if value:
                            values(v_before, value[1], i, value[2])
                        beside(i)

                def step(j):
                    s = b * NT + j
                    k = b * SPARE + spare(j)

                    if has_o(j) and not is_int(j, 1):
                        pe.wait_ge(x2_done, SUB * s - SUB - 1)
                    pe.wait_ge(spare_free[0], k + 1)
                    pe.wait_ge(max_done, blocks(pe, b, j + 1, 0))
                    for u in range(SUB):
                        ins = t_.transpose(ps_x[:, 0, u * P:(u + 1) * P], run_max[:, u * P:(u + 1) * P], ident[:, :])
                    ins.then_inc(maxT_psum, 1)

                    def max_row_back():
                        if has_o(j) and not is_int(j, 1):
                            pe.wait_ge(x2_done, SUB * s - SUB)
                        pe.wait_ge(spare_free[0], k + 2)
                        pe.wait_ge(spare_free[1], k + 1)
                        for u in range(SUB):
                            ins = t_.transpose(ps_x[:, 1, u * P:(u + 1) * P], max_col[:, u:u + 1].to_broadcast([P, P]),
                                               ident[:, :])
                        ins.then_inc(maxrow_psum, 1)

                    def first(i):
                        if i == 1:
                            max_row_back()
                        if is_int(j, 0) and i >= 2:
                            query(j + 2, k + 1, i - 2)

                    def first_pair(i):
                        if has_next(j, 2) and i < DC:
                            query(j + 2, k + 1, i)

                    def last_pair(i):
                        if is_int(j, 1):
                            first_pair(i)
                        if i >= 2:
                            output(s - 1, k + 1 + int(has_next(j, 2)), i - 2)

                    def diagonal(i):
                        if has_o(j) and 1 <= i <= 2:
                            output(s - 1, k + 1, i + 1)

                    if has_next(j, 1):
                        group((j + 1, 1, is_int(j, 0)), None, first)
                    else:
                        max_row_back()
                    wait_apart(pe, u_done, s + 1)
                    over_pairs(pe, j, lambda m: group((j + 1, m + 2, False) if has_next(j, 1) else None,
                                                      (j, m, False), first_pair if is_int(m, 0) else lambda i: None))
                    if has_o(j):
                        group((j + 1, j + 1, True) if has_next(j, 1) else None, (j, j - 1, False), last_pair)
                    group((j + 2, 0, False) if has_next(j, 2) else None, (j, j, True), diagonal)

                for j in range(2):
                    for c in range(DC):
                        query(j, b * SPARE + j, c)
                group((0, 0, True), None, lambda i: None)
                group((1, 0, False), None, lambda i: None)
                over_steps(pe, step)
                pe.wait_ge(x2_done, SUB * (b * NT + NT - 1))
                for u in range(SUB):
                    output(b * NT + NT - 1, b * SPARE + SPARE, u)

            with pe.Fori(0, B) as b:
                ffn(0, b)
                barrier(pe, after_ffn(0, b))
                attention_input(b)
                barrier(pe, after_ffn(0, b) + 1)
                attention(b)
                barrier(pe, after_ffn(0, b) + 2)
            with pe.Fori(0, B) as b:
                ffn(1, b)
                barrier(pe, after_ffn(1, b))


_INS = ["L0_attn_x", "L0_attn_Wq", "L0_attn_bq", "L0_attn_Wk", "L0_attn_bk", "L0_attn_Wv", "L0_attn_bv", "L0_attn_Wo",
        "L0_attn_bo", "L0_ffn_mix_kernel", "L0_ffn_W1", "L0_ffn_b1", "L0_ffn_W2", "L0_ffn_b2", "L0_ffn_Wo1",
        "L0_ffn_bo1", "L0_ffn_Wo2", "L0_ffn_bo2", "L0_ffn_gamma", "L0_ffn_beta"]


def kernel(**inputs):
    import numpy as _np
    import concourse.bacc as _bacc
    from concourse.bass_utils import run_bass_kernel_spmd as _run

    nc = _bacc.Bacc("TRN2", target_bir_lowering=False, num_devices=1)
    arrays, args = {}, []
    for name in _INS:
        a = _np.ascontiguousarray(inputs[name])
        arrays[f"in_{name}"] = a
        args.append(nc.dram_tensor(f"in_{name}", a.shape, mybir.dt.from_np(a.dtype), kind="ExternalInput").ap())
    out = nc.dram_tensor("out_0", (B, S, D), F32, kind="ExternalOutput").ap()
    macaron(nc, *args, out)
    r = _run(nc, [arrays], core_ids=[0])
    return r.results[0]["out_0"]
```

```python
import concourse.bass as bass
from concourse import mybir
from contextlib import ExitStack

F32 = mybir.dt.float32
F16 = mybir.dt.float16
ALU = mybir.AluOpType
ACT = mybir.ActivationFunctionType
AX = mybir.AxisListType

P = 128
B, S, D = 2, 4096, 256
NP, DM = 9, 64
DC = D // P
TT = 512
SUB = TT // P
NTT = B * S // TT
NT = S // TT
HC = (DM + NP * DM) // P
EPS = 1e-5

XS = 64.0
WS = 64.0
QS = 32.0
BETA = 1.0 / 16
P_LOG = 8.317766166719343
MASKED = -1e30

AHEAD = 5
SETS = 7
EARLY = 5
RING = 10


def macaron(nc, x, Wq, bq, Wk, bk, Wv, bv, Wo, bo, mix, W1, b1, W2, b2, Wo1, bo1, Wo2, bo2,
            gamma, beta, out):
    x1 = nc.dram_tensor("x1_scratch", (B, S, D), F32, kind="Internal").ap()
    x2 = nc.dram_tensor("x2_scratch", (B, S, D), F32, kind="Internal").ap()

    def tiles(a):
        return a.rearrange("b (t u p) d -> (b t) p u d", u=SUB, p=P)

    x_t, x1_t, x2_t, out_t = tiles(x), tiles(x1), tiles(x2), tiles(out)

    ctx = ExitStack()
    with ctx:
        def sb(name, shape, dt=F32):
            return ctx.enter_context(nc.sbuf_tensor(name, shape, dt))

        def sem(name):
            return ctx.enter_context(nc.semaphore(name))

        def cols(a, at, n):
            return a[:, bass.ds(at, n)]

        R1 = sb("R1", [P, RING * SUB * TT])
        R2 = sb("R2", [P, 16384])
        R3 = sb("R3", [P, NT * SUB * D])

        class Region:

            def __init__(self, tensor):
                self.tensor, self.at = tensor, 0

            def take(self, n, dt=F32):
                words = n if dt == F32 else n // 2
                part = self.tensor[:, self.at:self.at + words]
                self.at += words
                assert self.at <= self.tensor.shape[1]
                return part if dt == F32 else part.bitcast(dt)

        f1, f2 = Region(R1), Region(R2)
        NTC = S + 2
        nT = f1.take(DC * NTC)
        Ns = f1.take(SUB * D)
        N = R3[:, :]
        hb = f2.take(HC * TT)
        hm = f2.take(2 * TT)
        hhi = f2.take(HC * TT, F16)
        hlo = f2.take(HC * TT, F16)
        xa = f2.take(DC * TT)
        xm = f2.take(DC * TT)
        xhi = f2.take(2 * DC * TT, F16)
        xlo = f2.take(2 * DC * TT, F16)
        wqkv_s = f2.take(3 * DC * D)
        wo_s = f2.take(DC * D)
        wo_t = f2.take(DC * D)
        bqkv_s = f2.take(8)
        off_s = f2.take(8)
        b1_s = f2.take(8)
        w1_s = f1.take(DC * HC * P)
        w2_s = f1.take(HC * D)
        X_AT = (RING * SUB * TT) - NT * SUB * D
        assert f1.at <= X_AT
        X = R1[:, X_AT:]
        y = f2.take(SUB * D)
        z = f2.take(SUB * D)
        xb = f2.take(SUB * D)
        a1, a2, a3 = Region(R1), Region(R2), Region(R3)
        ring = a1.take(RING * SUB * TT)
        KT_hi = a2.take(DC * S, F16)
        KT_lo = a2.take(DC * S, F16)
        KV_hi = a2.take(S // P * D, F16)
        KV_lo = a2.take(S // P * D, F16)
        q_hi = a3.take(2 * DC * TT, F16)
        q_lo = a3.take(2 * DC * TT, F16)
        pf = a3.take(2 * TT)
        p_hi = a3.take(SUB * TT, F16)
        p_lo = a3.take(SUB * TT, F16)
        U = a3.take(DC * TT)
        xr = a3.take(SUB * D)
        rows_in = [cols(X, i * SUB * D, SUB * D) for i in range(EARLY)]
        rows_in += [a3.take(SUB * D)] * (NT - EARLY)
        xr_beside = rows_in[NT - 1]

        run_max = sb("run_max", [P, TT])
        max_row = sb("max_row", [P, TT])
        max_col = sb("max_col", [P, SUB])
        rden = sb("rden", [P, SUB])
        w1_hi = sb("w1_hi", [P, DC, HC * P], F16)
        w1_lo = sb("w1_lo", [P, DC, HC * P], F16)
        w2_hi = sb("w2_hi", [P, HC, D], F16)
        w2_lo = sb("w2_lo", [P, HC, D], F16)
        wqk_hi = sb("wqk_hi", [P, DC, D], F16)
        wqk_lo = sb("wqk_lo", [P, DC, D], F16)
        wvo = sb("wvo", [P, DC, D + 8])
        wo2 = sb("wo2", [DM + 1, NP])
        b1c = sb("b1c", [P, HC])
        bo1c = sb("bo1c", [DM, 1])
        kmix = sb("kmix", [P, DC, 3])
        gamma_b = sb("gamma_b", [P, D])
        beta_b = sb("beta_b", [P, D])
        bo_b = sb("bo_b", [P, D])
        ident = sb("ident", [P, P])
        ident16 = sb("ident16", [P, P], F16)
        tri = sb("tri", [P, P])
        expand = sb("expand", [NP, HC, P], F16)
        prio = sb("prio", [P, SUB, NP])
        half = sb("half", [P, SUB])
        th = sb("th", [DM + 1, TT])
        oh = sb("oh", [P, SUB, NP], F16)
        oh_t = sb("oh_t", [NP, TT], F16)
        r_max = sb("r_max", [P, SUB])
        r_eq = sb("r_eq", [P, SUB, NP])
        r_pr = sb("r_pr", [P, SUB, NP])
        r_top = sb("r_top", [P, SUB])
        st = sb("st", [P, SETS, SUB, 6])
        mv = sb("mv", [P, SETS, SUB, 2])
        rstd = sb("rstd", [P, SETS, SUB])
        veps = sb("veps", [P, SETS, SUB])
        neg = sb("neg", [P, SETS, SUB])
        shift = sb("shift", [P, SETS, SUB])
        key_rstd = sb("key_rstd", [P, EARLY, SUB])
        key_shift = sb("key_shift", [P, EARLY, SUB])
        PS = ctx.enter_context(nc.psum_tensor("PS", [P, 8, TT], F32))
        ps_h, ps_m, ps_o, ps_n = PS[:, 0:2, :], PS[:, 2:4, :], PS[:, 4:6, :], PS[:, 6, :]
        ps_route = PS[:, 7, 0:SUB * 16].rearrange("p (u e) -> p u e", u=SUB)[:, :, 0:NP]
        ps_oh = PS[:, 7, TT // 2:].bitcast(F16)
        ps_s, ps_u, ps_x = PS[:, 0:4, :], PS[:, 4:6, :], PS[:, 6:8, :]

        waited = sem("waited")
        weights_in, w2_cleared = sem("weights_in"), sem("w2_cleared")
        attention_weights_in = sem("attention_weights_in")
        pool_const, fold_step, folded, woT_psum = sem("pool_const"), sem("fold_step"), sem("folded"), sem("woT_psum")
        woT_done, wqk_psum, wvo_psum = sem("woT_done"), sem("wqk_psum"), sem("wvo_psum")
        x_first, x_in = [sem(f"x_first{i}") for i in range(AHEAD + 1)], sem("x_in")
        kmix_ready, weights_ready = sem("kmix_ready"), sem("weights_ready")
        n_stat, n_var, n_eps, n_rstd, n_neg, n_shift, n_done, n_kept, n_beside = (
            sem("n_" + s) for s in ("stat", "var", "eps", "rstd", "neg", "shift", "done", "kept", "beside"))
        r_stat, r_var, r_eps, r_rstd, r_mid = (sem("r_" + s) for s in ("stat", "var", "eps", "rstd", "mid"))
        r_neg, r_shift, z_done = sem("r_neg"), sem("r_shift"), sem("z_done")
        a_stat, a_var, a_eps, a_rstd, a_neg, a_part, a_shift, a_done = (
            sem("a_" + s) for s in ("stat", "var", "eps", "rstd", "neg", "part", "shift", "done"))
        nT_psum, nT_done, edges_set = sem("nT_psum"), sem("nT_done"), sem("edges_set")
        xa_done, mix_part, mix_done = sem("xa_done"), sem("mix_part"), sem("mix_done")
        xhi_done, xlo_done = sem("xhi_done"), sem("xlo_done")
        h_psum, hb_done, tanh_done = sem("h_psum"), sem("hb_done"), sem("tanh_done")
        route_psum, route_step, oh_done = sem("route_psum"), sem("route_step"), sem("oh_done")
        ohT_psum, ohT_done, mask_psum = sem("ohT_psum"), sem("ohT_done"), sem("mask_psum")
        hm_done, hhi_done, hlo_done = sem("hm_done"), sem("hhi_done"), sem("hlo_done")
        o_psum, y_done, xb_done, x1_done, stored = (sem("o_psum"), sem("y_done"), sem("xb_done"), sem("x1_done"),
                                                    sem("stored"))
        a_hi, a_lo, aT_psum, aT_hi, aT_lo = sem("a_hi"), sem("a_lo"), sem("aT_psum"), sem("aT_hi"), sem("aT_lo")
        q_psum, q_hi_done, spare_free = sem("q_psum"), sem("q_hi_done"), [sem("spare_free0"), sem("spare_free1")]
        s_psum, abs_done, tri_done, max_done = sem("s_psum"), sem("abs_done"), sem("tri_done"), sem("max_done")
        maxT_psum, maxrow_psum = sem("maxT_psum"), sem("maxrow_psum")
        sub_done, exp_done, phi_done, plo_done = sem("sub_done"), sem("exp_done"), sem("phi_done"), sem("plo_done")
        pv_done, u_done, out_psum, rden_done = sem("pv_done"), sem("u_done"), sem("out_psum"), sem("rden_done")
        a_in = sem("a_in")
        f_in = [sem(f"f_in{i}") for i in range(EARLY)]
        f_stat, f_var, f_eps, f_rstd, f_neg, f_shift, f_scaled = (
            sem("f_" + s) for s in ("stat", "var", "eps", "rstd", "neg", "shift", "scaled"))
        a_rows = [sem(f"a_rows{i}") for i in range(EARLY)]
        xr_in, x2_done, x2_stored = sem("xr_in"), sem("x2_done"), sem("x2_stored")

        block = ctx.enter_context(nc.Block())
        LOADS, ATTENTION_LOADS = 15, 8
        POOL_CONSTS = NP + 9

        def wait_apart(eng, semaphore, value):
            eng.wait_ge(semaphore, value)
            eng.sem_inc(waited, 1)

        def attention_over(eng):
            wait_apart(eng, x2_done, SUB * NTT)

        def slot(t):
            return t & (NT - 1)

        BLOCKS = SUB * NT * (NT + 1) // 2

        def within(eng, value, largest):
            if isinstance(value, int):
                return value
            return eng.snap(nc.s_assert_within(value, 0, largest, skip_runtime_bounds_check_because="loop bounds"))

        def blocks(eng, b, j, m):
            return within(eng, b * BLOCKS + 2 * (j * (j + 1)) + SUB * m, B * BLOCKS)

        def ring_at(eng, j, m):
            if isinstance(j, int) and isinstance(m, int):
                return (j * (j + 1) // 2 + m) % RING * (SUB * TT)
            return within(eng, (((j * (j + 1)) >> 1) + m) % RING * (SUB * TT), (RING - 1) * SUB * TT)

        def spare(j):
            return 2 * NT - 1 if is_int(j, NT - 1) else 2 + 2 * j
        SPARE = 2 * NT

        def has_next(j, n):
            return not isinstance(j, int) or j + n < NT

        KEYS = 3

        def has_keys(j):
            return not isinstance(j, int) or EARLY <= j + KEYS < NT

        def key_bank(t):
            return 4 if t % 2 == 0 else 0

        SPARE_BANK = 6

        def rows_wait(eng, b, t):
            if isinstance(t, int) and t < EARLY:
                eng.wait_ge(a_rows[t], b + 1)
            else:
                eng.wait_ge(a_done, b * (NT - EARLY) + t - EARLY + 1)

        def has_o(j):
            return not isinstance(j, int) or j >= 1

        def is_int(j, value):
            return isinstance(j, int) and j == value

        def rows4(a):
            return a.rearrange("p (u d) -> p u d", u=SUB)

        def dram_tile(a, i):
            return a[bass.ds(i, 1)].rearrange("a p u d -> p (a u) d")

        def over_steps(eng, step):
            for j in range(3):
                step(j)
            with eng.Fori(3, NT - 3) as j:
                step(j)
            for j in range(NT - 3, NT):
                step(j)

        def over_pairs(eng, j, pair):
            if isinstance(j, int) and j < 2:
                return
            pair(0)
            if not is_int(j, 2):
                with eng.Fori(1, j - 1) as m:
                    pair(m)

        def over_turns(eng, turn):
            for t in range(-AHEAD, 1):
                turn(t)
            with eng.Fori(1, NTT - AHEAD) as t:
                turn(t)
            for t in range(NTT - AHEAD, NTT + 1):
                turn(t)

        FIRST_SET = 2
        assert AHEAD == EARLY and FIRST_SET + EARLY == SETS

        def early(t):
            return isinstance(t, int) and t < AHEAD

        def rows_set(ph, t):
            if ph == 1 and early(t):
                return FIRST_SET + t
            return 3 if early(t) and t % 2 == 1 else 1

        def first_of(ph, t):
            k = t - (NTT - EARLY) if isinstance(t, int) else -1
            return [k] if ph == 0 and 0 <= k < EARLY else []

        def normal_rows(t):
            return cols(N, t * SUB * D, SUB * D) if early(t) else Ns

        def beside(ph, t):
            return {2: 1, 3: 2}.get(t) if ph == 1 and isinstance(t, int) else None

        def counted(ph, t):
            return ph * (NTT - EARLY) + t

        def rows_bank(t, c):
            return PS[:, 4, :] if early(t) and t < AHEAD - 1 and c == 1 else ps_n

        FOLD_STEPS = 4 + 2 * DC

        def is_tile(t):
            return not isinstance(t, int) or 0 <= t < NTT

        @block.sync
        def _(sp):
            def load(dst, src, columns=False):
                sp.dma_start(dst, src, allow_slow_non_contiguous=columns).then_inc(weights_in, 16)

            def load_weights():
                w1_v = w1_s.rearrange("p (c q m) -> p c q m", c=DC, m=DM)
                for c in range(DC):
                    load(kmix[:, c, :], mix[:, c * P:(c + 1) * P].rearrange("j p -> p j"), columns=True)
                load(w1_v[:, :, 0, :], Wo1.rearrange("(c p) m -> p c m", p=P))
                for c in range(DC):
                    load(w1_v[:, c, 1:, :], W1[:, c * P:(c + 1) * P, :].rearrange("e p m -> p e m"))
                w2_f = W2.rearrange("e m d -> (e m) d")
                w2_v = w2_s.rearrange("p (c d) -> p c d", c=HC)
                sp.wait_ge(w2_cleared, 1)
                load(w2_v[0:NP, 0, :], b2)
                load(w2_v[DM:P, 0, :], w2_f[0:DM, :])
                load(w2_v[:, 1:, :], w2_f[DM:, :].rearrange("(c p) d -> p c d", p=P))
                b1_f = b1.rearrange("e m -> (e m)")
                load(b1_s[DM:P, 0:1], b1_f[0:DM].rearrange("(p a) -> p a", a=1))
                load(b1_s[:, 1:HC], b1_f[DM:].rearrange("(c p) -> p c", p=P), columns=True)
                load(bo1c[:, :], bo1.rearrange("(p a) -> p a", a=1))
                load(wo2[0:DM, :], Wo2)
                load(wo2[DM:DM + 1, :], bo2.rearrange("(a e) -> a e", a=1))
                load(gamma_b[:, :], gamma.partition_broadcast(P))
                load(beta_b[:, :], beta.partition_broadcast(P))

            def load_attention_weights():
                def load(dst, src, columns=False):
                    sp.dma_start(dst, src, allow_slow_non_contiguous=columns).then_inc(attention_weights_in, 16)

                for i, w in enumerate((Wq, Wk, Wv)):
                    load(wqkv_s[:, i * DC * D:(i + 1) * DC * D].rearrange("p (c d) -> p c d", c=DC),
                         w.rearrange("(c p) d -> p c d", p=P))
                for i, bias in enumerate((bq, bk, bv)):
                    load(bqkv_s[:, DC * i:DC * i + DC], bias.rearrange("(c p) -> p c", p=P), columns=True)
                load(wo_s.rearrange("p (c d) -> p c d", c=DC), Wo.rearrange("(c p) d -> p c d", p=P))
                load(bo_b[:, :], bo.partition_broadcast(P))

            def ffn(ph, src, dst):
                g0 = ph * NTT

                def load_rows(t):
                    at = cols(X, slot(t) * SUB * D, SUB * D)
                    if isinstance(t, int) and t <= AHEAD:
                        sp.dma_start(rows4(at), dram_tile(src, t)).then_inc(x_first[t], 16)
                        return
                    n = ph * (NTT - AHEAD - 1) + t - AHEAD - 1
                    if not is_int(n, 0):
                        wait_apart(sp, x_in, 16 * n)
                    sp.dma_start(rows4(at), dram_tile(src, t)).then_inc(x_in, 16)

                def store(t):
                    wait_apart(sp, x1_done, g0 + t + 2)
                    wait_apart(sp, stored, 16 * (g0 + t + NT))
                    sp.dma_start(dram_tile(dst, t), rows4(cols(N, slot(t) * SUB * D, SUB * D))).then_inc(stored, 16)

                for t in range(NT) if ph == 0 else range(EARLY, NT):
                    load_rows(t)
                    if t == 2 and ph == 0:
                        load_weights()
                if ph == 0:
                    load_attention_weights()
                else:
                    sp.wait_ge(x2_stored, 16 * NTT + 1)
                store(0)
                load_rows(NT)
                with sp.Fori(1, NTT - NT) as t:
                    store(t)
                    load_rows(t + NT)
                if ph == 0:
                    for t in range(EARLY):
                        store(NTT - NT + t)
                        load_first(x1_t, 0, [t])
                with sp.Fori(NTT - NT + (EARLY if ph == 0 else 0), NTT) as t:
                    store(t)

            def load_first(src, i, tiles):
                for t in tiles:
                    sp.dma_start(rows4(rows_in[t]), dram_tile(src, i + t)).then_inc(f_in[t], 16)

            def attention(b):
                def load_keys(t):
                    sp.dma_start(rows4(rows_in[t]), dram_tile(x1_t, b * NT + t)).then_inc(a_in, 16)

                def load_residual(j, rows=xr):
                    s = b * NT + j
                    if rows is xr:
                        sp.wait_ge(x2_stored, 16 * (s - 1 if is_int(j, NT - 1) else s) + 1)
                    sp.dma_start(rows4(rows), dram_tile(x1_t, s)).then_inc(xr_in, 16)

                def store(j, rows=xr):
                    s = b * NT + j
                    sp.wait_ge(x2_done, SUB * s + SUB)
                    sp.dma_start(dram_tile(x2_t, s), rows4(rows)).then_inc(x2_stored, 16)

                sp.wait_ge(stored, 16 * (NTT + NT))
                sp.wait_ge(x2_stored, 16 * (b * NT) + 1)
                load_keys(EARLY)
                load_residual(0)
                store(0)
                load_residual(1)
                for t in range(EARLY + 1, NT):
                    sp.wait_ge(aT_lo, DC * (b * NT + t) + DC)
                    sp.wait_ge(a_lo, b * NT + t)
                    load_keys(t)
                    store(t - EARLY)
                    load_residual(t - EARLY + 1)
                with sp.Fori(NT - EARLY, NT - 3) as j:
                    store(j)
                    load_residual(j + 1)
                sp.wait_ge(aT_lo, DC * (b * NT + NT) + DC)
                sp.wait_ge(a_lo, b * NT + NT)
                sp.wait_ge(xr_in, 16 * (b * NT + NT - 2))
                load_residual(NT - 2, xr_beside)
                store(NT - 3)
                sp.wait_ge(xr_in, 16 * (b * NT + NT - 1))
                load_residual(NT - 1)
                first = (x1_t, (b + 1) * NT) if b + 1 < B else (x2_t, 0)
                sp.wait_ge(pv_done, blocks(sp, b, NT - 1, 0) + SUB)
                load_first(*first, range(EARLY - 1))
                store(NT - 2, xr_beside)
                sp.wait_ge(pv_done, blocks(sp, b, NT - 1, 1) + SUB)
                load_first(*first, range(EARLY - 1, EARLY))
                store(NT - 1)

            sp.sem_inc(x2_stored, 1)
            sp.sem_inc(stored, 16 * NT)
            ffn(0, x_t, x1_t)
            for b in range(B):
                attention(b)
            ffn(1, x2_t, out_t)
            sp.wait_ge(stored, 16 * (2 * NTT + NT))

        @block.gpsimd
        def _(pool):
            g = nc.gpsimd
            g.memset(th[DM:DM + 1, :], 1.0).then_inc(pool_const, 1)
            pool.wait_ge(pool_const, 1)
            g.memset(ident[:, :], 0.0).then_inc(pool_const, 1)
            g.memset(tri[:, :], 0.0).then_inc(pool_const, 1)
            g.memset(expand[:, :, :], 1.0).then_inc(pool_const, 1)
            g.memset(half[:, :], -0.5).then_inc(pool_const, 1)
            for e in range(NP):
                g.memset(prio[:, :, e:e + 1], float(NP - e)).then_inc(pool_const, 1)
            pool.wait_ge(pool_const, NP + 5)
            g.affine_select(out=ident[:, :], in_=ident[:, :], compare_op=ALU.not_equal, fill=1.0,
                            base=0, pattern=[[-1, P]], channel_multiplier=1).then_inc(pool_const, 1)
            g.affine_select(out=tri[:, :], in_=tri[:, :], compare_op=ALU.is_ge, fill=MASKED,
                            base=0, pattern=[[1, P]], channel_multiplier=-1).then_inc(pool_const, 1)
            expand_v = expand[:, :, :].rearrange("e c (k m) -> e (c k) m", m=DM)
            g.affine_select(out=expand_v, in_=expand_v, compare_op=ALU.is_equal, fill=0.0, base=-1,
                            pattern=[[1, 2 * HC], [0, DM]], channel_multiplier=-1).then_inc(pool_const, 1)
            pool.wait_ge(pool_const, NP + 8)
            g.affine_select(out=expand[:, 0, 0:DM], in_=expand[:, 0, 0:DM], compare_op=ALU.not_equal, fill=1.0,
                            base=0, pattern=[[-1, DM]], channel_multiplier=1).then_inc(pool_const, 1)

            def inverse_root(var_ready, eps_done, rstd_done, i, value, scale=1.0):
                wait_apart(pool, var_ready, value)
                g.tensor_scalar(veps[:, i, :], mv[:, i, :, 1], scale ** -2, EPS * scale ** -2, ALU.mult, ALU.add)\
                    .then_inc(eps_done, 1)
                pool.wait_ge(eps_done, value)
                g.tensor_tensor(rstd[:, i, :], veps[:, i, :], half[:, :], ALU.pow).then_inc(rstd_done, 1)

            def norm_scale(value, i, sems, scale=1.0):
                var_ready, eps_done, rstd_done, neg_done, shift_done = sems
                inverse_root(var_ready, eps_done, rstd_done, i, value, scale)
                g.tensor_scalar(neg[:, i, :], mv[:, i, :, 0], -1.0, None, ALU.mult).then_inc(neg_done, 1)
                wait_apart(pool, neg_done, value)
                pool.wait_ge(rstd_done, value)
                g.tensor_tensor(shift[:, i, :], neg[:, i, :], rstd[:, i, :], ALU.mult).then_inc(shift_done, 1)

            def ffn(ph):
                g0 = ph * NTT

                def result(t):
                    pool.wait_ge(z_done, g0 + t + 1)
                    g.tensor_tensor(rows4(z), rows4(z), gamma_b[:, :].unsqueeze(1).to_broadcast([P, SUB, D]),
                                    ALU.mult).then_inc(r_mid, 1)
                    pool.wait_ge(r_mid, g0 + t + 1)
                    pool.wait_ge(xb_done, g0 + t + 1)
                    g.tensor_tensor(cols(N, slot(t) * SUB * D, SUB * D), z, xb, ALU.add).then_inc(x1_done, 1)

                def turn(t):
                    if ph == 0 and is_int(t, 0):
                        wait_apart(pool, weights_ready, 2)
                    if is_tile(t - 1):
                        norm_scale(g0 + t, 0, (r_var, r_eps, r_rstd, r_neg, r_shift))
                    if is_tile(t - 1) and not is_int(t, NTT):
                        result(t - 1)
                    if is_tile(t):
                        pool.wait_ge(x1_done, g0 + t + 1)
                        g.tensor_tensor(rows4(xb), rows4(cols(X, slot(t) * SUB * D, SUB * D)),
                                        beta_b[:, :].unsqueeze(1).to_broadcast([P, SUB, D]), ALU.add)\
                            .then_inc(xb_done, 1)
                    if is_tile(t + AHEAD) and not (ph == 1 and early(t + AHEAD)):
                        if early(t + AHEAD):
                            if t + AHEAD >= 2:
                                pool.wait_ge(n_done, g0 + t + AHEAD - 1)
                        else:
                            pool.wait_ge(n_done, g0 + t + AHEAD)
                        norm_scale(counted(ph, t + AHEAD + 1), rows_set(ph, t + AHEAD),
                                   (n_var, n_eps, n_rstd, n_neg, n_shift))
                    elif first_of(ph, t):
                        first_scales(0, first_of(ph, t))

                over_turns(pool, turn)
                if ph == 0:
                    result(NTT - 1)

            def attention(b):
                def key_scale(t, i):
                    if t > EARLY:
                        pool.wait_ge(a_done, b * (NT - EARLY) + t - EARLY)
                    value = b * (NT - EARLY) + t - EARLY + 1
                    norm_scale(value, i, (a_var, a_eps, a_rstd, a_neg, a_part), scale=XS)
                    wait_apart(pool, a_part, value)
                    g.tensor_scalar(shift[:, i, :], shift[:, i, :], XS * BETA, None, ALU.add).then_inc(a_shift, 1)

                def key_low(t):
                    pool.wait_ge(a_hi, b * NT + t + 1)
                    g.tensor_tensor(cols(KV_lo, t * SUB * D, SUB * D), rows_in[t], cols(KV_hi, t * SUB * D, SUB * D),
                                    ALU.subtract).then_inc(a_lo, 1)

                pool.wait_ge(x1_done, NTT + 1)
                pool.wait_ge(pv_done, b * BLOCKS + SUB)
                for t in range(EARLY):
                    key_low(t)
                for t in range(EARLY, NT):
                    key_scale(t, FIRST_SET)
                    key_low(t)
                first_scales(b + 1, range(EARLY))

            def first_scales(n, tiles):
                for t in tiles:
                    value, i = n * EARLY + t + 1, FIRST_SET + t
                    norm_scale(value, i, (f_var, f_eps, f_rstd, f_neg, f_shift))
                    g.tensor_scalar(key_rstd[:, t, :], rstd[:, i, :], XS, None, ALU.mult)
                    wait_apart(pool, f_shift, value)
                    g.tensor_scalar(key_shift[:, t, :], shift[:, i, :], XS, XS * BETA, ALU.mult, ALU.add)\
                        .then_inc(f_scaled, 1)

            ffn(0)
            with pool.Fori(0, B) as b:
                attention(b)
            attention_over(pool)
            ffn(1)

        @block.vector
        def _(dve):
            v = nc.vector
            v.memset(w2_s[:, 0:D], 0.0).then_inc(w2_cleared, 1)

            def prepare_first():
                w1h, w1l = (w[:, :, :].rearrange("p a b -> p (a b)") for w in (w1_hi, w1_lo))
                dve.wait_ge(weights_in, 16 * LOADS)
                v.tensor_scalar(kmix[:, :, :], kmix[:, :, :], XS, None, ALU.mult).then_inc(kmix_ready, 1)
                v.tensor_scalar(w1h, w1_s, WS, None, ALU.mult).then_inc(fold_step, 1)
                v.tensor_scalar(b1c[:, 1:HC], b1_s[:, 1:HC], XS, None, ALU.mult)
                v.tensor_scalar(b1c[DM:P, 0:1], b1_s[DM:P, 0:1], XS, None, ALU.mult)
                dve.wait_ge(pool_const, POOL_CONSTS)
                v.tensor_copy(ident16[:, :], ident[:, :])
                dve.wait_ge(fold_step, 1)
                v.scalar_tensor_tensor(out=w1l, in0=w1_s, scalar=WS, in1=w1h, op0=ALU.mult, op1=ALU.subtract)\
                    .then_inc(weights_ready, 1)
                dve.wait_ge(kmix_ready, 1)

            def prepare_second():
                w2h, w2l = (w[:, :, :].rearrange("p a b -> p (a b)") for w in (w2_hi, w2_lo))
                v.tensor_scalar(w2h, w2_s, WS, None, ALU.mult).then_inc(fold_step, 1)
                v.tensor_scalar(gamma_b[:, :], gamma_b[:, :], 0.5, None, ALU.mult)
                v.tensor_scalar(beta_b[:, :], beta_b[:, :], 0.5, None, ALU.mult)
                dve.wait_ge(fold_step, 2)
                v.scalar_tensor_tensor(out=w2l, in0=w2_s, scalar=WS, in1=w2h, op0=ALU.mult, op1=ALU.subtract)\
                    .then_inc(weights_ready, 1)

            def fold_biases():
                dve.wait_ge(attention_weights_in, 16 * ATTENTION_LOADS)
                v.tensor_reduce(off_s[:, 0:3 * DC], wqkv_s.rearrange("p (i d) -> p i d", d=D), AX.X, ALU.add)
                v.tensor_scalar(bqkv_s[:, 0:3 * DC], bqkv_s[:, 0:3 * DC], 1.0 / (D * BETA), None, ALU.mult)\
                    .then_inc(fold_step, 1)
                dve.wait_ge(fold_step, 3)
                v.scalar_tensor_tensor(out=off_s[:, 0:3 * DC], in0=off_s[:, 0:3 * DC], scalar=-1.0 / D,
                                       in1=bqkv_s[:, 0:3 * DC], op0=ALU.mult, op1=ALU.add).then_inc(fold_step, 1)
                dve.wait_ge(fold_step, 4)
                for i in range(3 * DC):
                    v.tensor_scalar(cols(wqkv_s, i * D, D), cols(wqkv_s, i * D, D), off_s[:, i:i + 1], None, ALU.add)\
                        .then_inc(folded, 1)
                v.memset(wvo[:, :, D:D + 8], 1.0 / (D * BETA))

            def fold_products():
                dve.wait_ge(woT_psum, 1)
                v.tensor_copy(wo_t, PS[:, 6, :]).then_inc(woT_done, 1)
                dve.wait_ge(wqk_psum, 1)
                for c in range(DC):
                    v.tensor_scalar(wqk_hi[:, c, :], PS[:, c, 0:D], WS, None, ALU.mult).then_inc(fold_step, 1)
                dve.wait_ge(fold_step, 4 + DC)
                for c in range(DC):
                    v.scalar_tensor_tensor(out=wqk_lo[:, c, :], in0=PS[:, c, 0:D], scalar=WS, in1=wqk_hi[:, c, :],
                                           op0=ALU.mult, op1=ALU.subtract)
                dve.wait_ge(wvo_psum, 1)
                for c in range(DC):
                    v.scalar_tensor_tensor(out=wvo[:, c, 0:D], in0=bo_b[:, :], scalar=1.0 / (D * BETA),
                                           in1=PS[:, 2 + c, 0:D], op0=ALU.mult, op1=ALU.add).then_inc(fold_step, 1)

            dve.sem_inc(x1_done, 1)
            dve.sem_inc(y_done, 2)
            dve.sem_inc(hm_done, 2)
            dve.sem_inc(aT_lo, DC)
            dve.sem_inc(plo_done, 2)
            dve.sem_inc(spare_free[0], 1)
            dve.sem_inc(spare_free[1], 1)

            def row_sums(src, at, i, stat_done):
                for u in range(SUB):
                    ins = v.bn_stats(st[:, i, u, :], cols(src, at + u * D, D))
                ins.then_inc(stat_done, 1)

            def row_moments(i, stat_done, var_done, value):
                wait_apart(dve, stat_done, value)
                for u in range(SUB):
                    ins = v.bn_aggr(mv[:, i, u, :], st[:, i, u, :])
                ins.then_inc(var_done, 1)

            def first_stats(n, tiles):
                for t in tiles:
                    dve.wait_ge(f_in[t], 16 * n + 16)
                    row_sums(X, t * SUB * D, FIRST_SET + t, f_stat)
                    row_moments(FIRST_SET + t, f_stat, f_var, n * EARLY + t + 1)

            def ffn(ph):
                g0 = ph * NTT
                nT_v = nT.rearrange("p (c s) -> p c s", c=DC)
                v.memset(nT_v[:, :, 0:1], 0.0)
                v.memset(nT_v[:, :, S + 1:S + 2], 0.0)
                v.memset(hb[0:DM, 0:TT], XS).then_inc(edges_set, 1)

                dve.wait_ge(edges_set, ph + 1)

                def input_sums(t):
                    if isinstance(t, int) and t <= AHEAD:
                        dve.wait_ge(x_first[t], 16 * (ph + 1))
                    else:
                        dve.wait_ge(x_in, 16 * (ph * (NTT - AHEAD - 1) + t - AHEAD))
                    if early(t):
                        if t >= 2:
                            dve.wait_ge(n_shift, counted(ph, t - 1))
                    else:
                        dve.wait_ge(n_shift, counted(ph, t))
                    row_sums(X, slot(t) * SUB * D, rows_set(ph, t), n_stat)

                def normalised(t):
                    dve.wait_ge(f_shift, B * EARLY + t + 1)
                    for u in range(SUB):
                        ins = v.tensor_scalar(cols(normal_rows(t), u * D, D), cols(X, (t * SUB + u) * D, D),
                                              rstd[:, rows_set(ph, t), u:u + 1], shift[:, rows_set(ph, t), u:u + 1],
                                              ALU.mult, ALU.add)
                    ins.then_inc(n_beside, 1)

                def input_moments(t):
                    row_moments(rows_set(ph, t), n_stat, n_var, counted(ph, t + 1))

                def mixed_before(t, c):
                    dve.wait_ge(xa_done, DC * (g0 + t) + c + 1)
                    v.scalar_tensor_tensor(out=cols(xm, c * TT, TT), in0=cols(nT, c * NTC + slot(t) * TT, TT),
                                           scalar=kmix[:, c, 0:1], in1=cols(xa, c * TT, TT), op0=ALU.mult, op1=ALU.add)\
                        .then_inc(mix_part, 1)

                def mixed_behind(t, c):
                    dve.wait_ge(mix_part, DC * (g0 + t) + c + 1)
                    v.scalar_tensor_tensor(out=cols(xm, c * TT, TT), in0=cols(nT, c * NTC + slot(t) * TT + 2, TT),
                                           scalar=kmix[:, c, 2:3], in1=cols(xm, c * TT, TT), op0=ALU.mult, op1=ALU.add)\
                        .then_inc(mix_done, 1)

                def mixed_low(t):
                    for c in range(DC):
                        dve.wait_ge(xhi_done, DC * (g0 + t) + c + 1)
                        at = (t & 1) * (DC * TT) + c * TT
                        v.tensor_tensor(cols(xlo, at, TT), cols(xm, c * TT, TT), cols(xhi, at, TT),
                                        ALU.subtract).then_inc(xlo_done, 1)

                def result(t):
                    dve.wait_ge(o_psum, g0 + t + 1)
                    dve.wait_ge(n_kept, g0 + t + 1)
                    if not is_int(t, 0):
                        dve.wait_ge(z_done, g0 + t)
                    for i in range(2):
                        v.scalar_tensor_tensor(out=cols(y, i * TT, TT), in0=ps_o[:, i, :], scalar=1.0 / (XS * WS),
                                               in1=cols(N, slot(t) * SUB * D + i * TT, TT), op0=ALU.mult, op1=ALU.add)\
                            .then_inc(y_done, 1)

                def result_sums(t):
                    dve.wait_ge(y_done, 2 * (g0 + t) + 4)
                    row_sums(y, 0, 0, r_stat)

                def route(t, step):
                    k = 4 * (g0 + t)
                    if step == 0:
                        dve.wait_ge(route_psum, g0 + t + 1)
                        v.tensor_reduce(r_max[:, :], ps_route, AX.X, ALU.max).then_inc(route_step, 1)
                    if step == 1:
                        dve.wait_ge(route_step, k + 1)
                        v.tensor_tensor(r_eq[:, :, :], ps_route, r_max[:, :].unsqueeze(2).to_broadcast([P, SUB, NP]),
                                        ALU.is_equal).then_inc(route_step, 1)
                    if step == 2:
                        dve.wait_ge(route_step, k + 2)
                        v.tensor_tensor(r_pr[:, :, :], r_eq[:, :, :], prio[:, :, :], ALU.mult).then_inc(route_step, 1)
                    if step == 3:
                        dve.wait_ge(route_step, k + 3)
                        v.tensor_reduce(r_top[:, :], r_pr[:, :, :], AX.X, ALU.max).then_inc(route_step, 1)
                    if step == 4:
                        dve.wait_ge(route_step, k + 4)
                        v.tensor_tensor(oh[:, :, :], r_pr[:, :, :], r_top[:, :].unsqueeze(2).to_broadcast([P, SUB, NP]),
                                        ALU.is_equal).then_inc(oh_done, 1)

                def masked(t, c):
                    k = HC * (g0 + t) + c
                    dve.wait_ge(hb_done, k + 3)
                    if c >= 2 or not is_int(t, 0):
                        dve.wait_ge(hlo_done, k if c == 0 else k - 1)
                    dve.wait_ge(mask_psum, k + 1)
                    v.tensor_tensor(cols(hm, (c % 2) * TT, TT), ps_m[:, c % 2, :], cols(hb, c * TT, TT), ALU.mult)\
                        .then_inc(hm_done, 1)

                def masked_low(t, c):
                    dve.wait_ge(hhi_done, HC * (g0 + t) + c + 1)
                    v.tensor_tensor(cols(hlo, c * TT, TT), cols(hm, (c % 2) * TT, TT), cols(hhi, c * TT, TT),
                                    ALU.subtract).then_inc(hlo_done, 1)

                def turn(t):
                    second, choice, mix, normal = is_tile(t), is_tile(t + 1), is_tile(t + 2), is_tile(t - 1)
                    rows = is_tile(t + AHEAD) and not (ph == 1 and early(t + AHEAD))
                    if ph == 0 and is_int(t, -2):
                        prepare_first()
                    if ph == 0 and is_int(t, -1):
                        prepare_second()
                    if beside(ph, t + 4):
                        normalised(t + 4)
                    if normal:
                        result(t - 1)
                    if second:
                        masked(t, 2)
                        masked_low(t, 1)
                    if normal:
                        result_sums(t - 1)
                    if second:
                        masked(t, 3)
                    if normal:
                        row_moments(0, r_stat, r_var, g0 + t)
                    if second:
                        masked_low(t, 2)
                    for step in range(5):
                        if choice:
                            route(t + 1, step)
                        if mix and step < 2:
                            mixed_before(t + 2, step)
                        elif mix and step < 4:
                            mixed_behind(t + 2, step - 2)
                    if ph == 0 and is_int(t, NTT - 2):
                        fold_biases()
                    if second:
                        masked(t, 4)
                        masked_low(t, 3)
                    if rows:
                        input_sums(t + AHEAD)
                    elif first_of(ph, t):
                        first_stats(0, first_of(ph, t))
                    if second:
                        masked_low(t, 4)
                    if rows:
                        input_moments(t + AHEAD)
                    if mix:
                        mixed_low(t + 2)
                    if choice:
                        masked(t + 1, 0)
                        masked(t + 1, 1)
                        masked_low(t + 1, 0)

                over_turns(dve, turn)
                if ph == 0:
                    fold_products()
                dve.wait_ge(r_shift, g0 + NTT)
                for u in range(SUB):
                    ins = v.tensor_scalar(cols(z, u * D, D), cols(y, u * D, D), rstd[:, 0, u:u + 1],
                                          shift[:, 0, u:u + 1], ALU.mult, ALU.add)
                ins.then_inc(z_done, 1)
                if ph == 1:
                    dve.wait_ge(z_done, g0 + NTT)
                    dve.wait_ge(xb_done, g0 + NTT)
                    v.tensor_tensor(rows4(z), rows4(z), gamma_b[:, :].unsqueeze(1).to_broadcast([P, SUB, D]),
                                    ALU.mult).then_inc(r_mid, 1)
                    dve.wait_ge(r_mid, g0 + NTT)
                    v.tensor_tensor(cols(N, slot(NTT - 1) * SUB * D, SUB * D), z, xb, ALU.add).then_inc(x1_done, 1)

            def attention(b):
                def key_stats(t, i):
                    n = b * (NT - EARLY) + t - EARLY
                    dve.wait_ge(a_in, 16 * n + 16)
                    if not isinstance(t, int) or t > EARLY:
                        dve.wait_ge(a_shift, n)
                    row_sums(rows_in[NT - 1], 0, i, a_stat)
                    row_moments(i, a_stat, a_var, n + 1)

                def key_rows(t):
                    rows = rows_in[t]
                    dve.wait_ge(f_scaled, b * EARLY + t + 1)
                    for u in range(SUB):
                        ins = v.tensor_scalar(cols(rows, u * D, D), cols(rows, u * D, D), key_rstd[:, t, u:u + 1],
                                              key_shift[:, t, u:u + 1], ALU.mult, ALU.add)
                    ins.then_inc(a_rows[t], 1)

                def keyT_low(t, c, bank):
                    dve.wait_ge(aT_hi, DC * (b * NT + t) + c + 1)
                    v.tensor_tensor(cols(KT_lo, c * S + t * TT, TT), PS[:, bank + c, :],
                                    cols(KT_hi, c * S + t * TT, TT), ALU.subtract).then_inc(aT_lo, 1)

                def key_lows(t):
                    for c in range(DC):
                        keyT_low(t, c, key_bank(t))

                def q_low(j, c):
                    dve.wait_ge(q_hi_done, DC * (b * NT + j) + c + 1)
                    at = (j & 1) * (DC * TT) + c * TT
                    v.scalar_tensor_tensor(out=cols(q_lo, at, TT), in0=ps_x[:, c, :], scalar=QS / (XS * WS),
                                           in1=cols(q_hi, at, TT), op0=ALU.mult, op1=ALU.subtract)\
                        .then_inc(spare_free[c], 1)

                def score_max(j, m, i, diagonal, before, ring_m):
                    n = before + i
                    lo = i * P if diagonal else 0
                    at = ring_m + i * TT + lo
                    dve.wait_ge(abs_done, n + SUB + 1)
                    if diagonal:
                        v.tensor_tensor(cols(ring, at, P), cols(ring, at, P), tri[:, :], ALU.add)\
                            .then_inc(tri_done, 1)
                        dve.wait_ge(tri_done, SUB * (b * NT + j) + i + 1)
                    if isinstance(m, int) and m == 0 and i == 0:
                        v.tensor_copy(run_max[:, :], cols(ring, at, TT)).then_inc(max_done, 1)
                    else:
                        dve.wait_ge(max_done, n)
                        v.tensor_tensor(run_max[:, lo:], run_max[:, lo:], cols(ring, at, TT - lo), ALU.max)\
                            .then_inc(max_done, 1)

                def shifted(i, diagonal, ring_n):
                    lo = i * P if diagonal else 0
                    at = ring_n + i * TT + lo
                    v.tensor_tensor(cols(ring, at, TT - lo), cols(ring, at, TT - lo), max_row[:, lo:], ALU.subtract)\
                        .then_inc(sub_done, 1)

                def p_low(i, diagonal, before):
                    lo = i * P if diagonal else 0
                    dve.wait_ge(phi_done, before + i + 1)
                    v.tensor_tensor(p_lo[:, i * TT + lo:(i + 1) * TT], pf[:, (i % 2) * TT + lo:(i % 2 + 1) * TT],
                                    p_hi[:, i * TT + lo:(i + 1) * TT], ALU.subtract).then_inc(plo_done, 1)

                def output(s, u, rows=xr):
                    if u == 0:
                        dve.wait_ge(xr_in, 16 * s + 16)
                    dve.wait_ge(out_psum, SUB * s + u + 1)
                    v.reciprocal(rden[:, u:u + 1], ps_x[:, u % 2, D:D + 1]).then_inc(rden_done, 1)
                    dve.wait_ge(rden_done, SUB * s + u + 1)
                    v.scalar_tensor_tensor(out=cols(rows, u * D, D), in0=ps_x[:, u % 2, 0:D],
                                           scalar=rden[:, u:u + 1], in1=cols(rows, u * D, D),
                                           op0=ALU.mult, op1=ALU.add).then_inc(x2_done, 1)

                def superblock(j, m, diagonal):
                    before, ring_m = blocks(dve, b, j, m), ring_at(dve, j, m)
                    return [(j, m, i, diagonal, before, ring_m) for i in range(SUB)]

                def one_by_one(j, m, diagonal):
                    return [[x] for x in superblock(j, m, diagonal)]

                def group(maxima, value, beside):
                    if value:
                        v_before, v_ring = blocks(dve, b, *value[:2]), ring_at(dve, *value[:2])
                    for i in range(SUB):
                        if value:
                            if i == 0 and is_int(value[1], 0):
                                dve.wait_ge(spare_free[1], b * SPARE + spare(value[0]) + 2)
                            shifted(i, value[2], v_ring)
                            if i >= 1:
                                p_low(i - 1, value[2], v_before)
                            elif not is_int(value[1], 0):
                                p_low(SUB - 1, False, v_before - SUB)
                        for maximum in maxima[i] if maxima else []:
                            score_max(*maximum)
                        beside(i)
                    if value and value[2]:
                        p_low(SUB - 1, True, v_before)
                    beside(SUB)

                def step(j):
                    s = b * NT + j
                    late = not isinstance(j, int) or j >= 2
                    if has_keys(j):
                        key_stats(j + KEYS, FIRST_SET)
                    dve.wait_ge(maxT_psum, s + 1)
                    v.tensor_reduce(max_col[:, :], rows4(ps_x[:, 0, :]), AX.X, ALU.max).then_inc(spare_free[0], 1)

                    def first(i):
                        if is_int(j, 0) and i == SUB:
                            for c in range(DC):
                                q_low(j + 2, c)

                    def last_pair(i):
                        if has_next(j, 2):
                            if is_int(j, 1) and i in (2, 3):
                                q_low(j + 2, i - 2)
                            if not is_int(j, 1) and i < DC:
                                q_low(j + 2, i)
                        if has_keys(j) and i == 3:
                            keyT_low(j + KEYS, 0, SPARE_BANK)

                    def diagonal(i):
                        if has_keys(j) and i == 0:
                            keyT_low(j + KEYS, 1, SPARE_BANK)
                        if has_o(j) and not is_int(j, NT - 1) and i >= 1:
                            output(s - 1, i - 1)

                    def first_pair(i):
                        if is_int(j, NT - 1):
                            for u in ((), (0, 1), (2,), (3,), ())[i]:
                                output(s - 1, u, xr_beside)

                    more, nxt = has_next(j, 1), j + 1

                    def pair(m):
                        if not more:
                            maxima = []
                        elif is_int(m, 0):
                            x = superblock(nxt, 1, False)
                            maxima = [begun[2:3], [begun[3], x[0]], x[1:3], x[3:]]
                        else:
                            maxima = one_by_one(nxt, m + 1, False)
                        group(maxima, (j, m, False), first_pair if is_int(m, 0) else lambda i: None)

                    if more:
                        begun = superblock(nxt, 0, False)
                        group([[x] for x in begun[:2]] + [[], []] if late else [[x] for x in begun], None, first)
                    over_pairs(dve, j, pair)
                    if has_o(j):
                        group(one_by_one(nxt, j, False) if more else [], (j, j - 1, False), last_pair)
                    group(one_by_one(nxt, nxt, True) if more else [], (j, j, True), diagonal)

                for t in range(EARLY - 1):
                    key_lows(t)
                    if t in (1, 2):
                        for c in range(DC):
                            q_low(t - 1, c)
                    if t < 2:
                        key_rows(EARLY - 2 + t)
                group(one_by_one(0, 0, True), None, lambda i: None)
                key_lows(EARLY - 1)
                over_steps(dve, step)
                first_stats(b + 1, range(1))
                for u in range(SUB):
                    output(b * NT + NT - 1, u)
                first_stats(b + 1, range(1, EARLY))

            ffn(0)
            with dve.Fori(0, B) as b:
                attention(b)
            ffn(1)

        @block.scalar
        def _(act):
            a = nc.scalar
            act.sem_inc(nT_done, 1)
            act.sem_inc(hb_done, 2)
            act.sem_inc(abs_done, SUB)
            act.sem_inc(u_done, 1)

            def ffn(ph):
                g0 = ph * NTT

                def normalised(t):
                    if beside(ph, t):
                        return
                    if not early(t):
                        act.wait_ge(n_kept, g0 + t)
                    if ph == 1 and early(t):
                        act.wait_ge(f_shift, B * EARLY + t + 1)
                    else:
                        act.wait_ge(n_shift, counted(ph, t + 1))
                    for u in range(SUB):
                        ins = a.activation(cols(normal_rows(t), u * D, D), cols(X, slot(t) * SUB * D + u * D, D), ACT.Identity,
                                           bias=shift[:, rows_set(ph, t), u:u + 1],
                                           scale=rstd[:, rows_set(ph, t), u:u + 1])
                    ins.then_inc(n_done, 1)

                def transposed(t, c):
                    act.wait_ge(nT_psum, DC * (g0 + t) + c + 1)
                    a.activation(cols(nT, c * NTC + slot(t) * TT + 1, TT), rows_bank(t, c), ACT.Copy).then_inc(nT_done, 1)

                def keep(t):
                    if ph == 1 and is_int(t, AHEAD - 1):
                        act.wait_ge(x2_stored, 16 * NTT + 1)
                    if early(t):
                        if beside(ph, t):
                            act.wait_ge(n_beside, beside(ph, t))
                            act.sem_inc(n_done, 1)
                        act.wait_ge(n_done, g0 + t + 1)
                        act.sem_inc(n_kept, 1)
                        return
                    act.wait_ge(n_done, g0 + t + 1)
                    act.wait_ge(stored, 16 * (g0 + t) + 16)
                    a.activation(cols(N, slot(t) * SUB * D, SUB * D), Ns, ACT.Copy).then_inc(n_kept, 1)

                def middle(t):
                    for c in range(DC):
                        if not is_int(t, 0):
                            act.wait_ge(mix_part, DC * (g0 + t))
                        act.wait_ge(nT_done, DC * (g0 + t) + c + 2)
                        a.activation(cols(xa, c * TT, TT), cols(nT, c * NTC + slot(t) * TT + 1, TT), ACT.Copy,
                                     scale=kmix[:, c, 1:2]).then_inc(xa_done, 1)

                def x_high(t):
                    for c in range(DC):
                        act.wait_ge(mix_done, DC * (g0 + t) + c + 1)
                        a.activation(cols(xhi, (t & 1) * (DC * TT) + c * TT, TT), cols(xm, c * TT, TT), ACT.Copy)\
                            .then_inc(xhi_done, 1)

                def hidden(t, c):
                    k = HC * (g0 + t) + c
                    act.wait_ge(h_psum, k + 1)
                    if c == 0:
                        a.activation(th[0:DM, :], ps_h[0:DM, 0, :], ACT.Tanh, bias=bo1c[:, :], scale=1.0 / (XS * WS))\
                            .then_inc(tanh_done, 1)
                    if not is_int(t, 0):
                        act.wait_ge(hm_done, k - HC + 3)
                    rows = slice(DM if c == 0 else 0, P)
                    a.activation(hb[rows, c * TT:(c + 1) * TT], ps_h[rows, c % 2, :], ACT.Identity,
                                 bias=b1c[rows, c:c + 1], scale=1.0 / WS).then_inc(hb_done, 1)

                def one_hot(t):
                    act.wait_ge(ohT_psum, g0 + t + 1)
                    a.activation(oh_t[:, :], ps_oh[0:NP, 0:TT], ACT.Copy).then_inc(ohT_done, 1)

                def masked_high(t, c):
                    act.wait_ge(hm_done, HC * (g0 + t) + c + 3)
                    a.activation(cols(hhi, c * TT, TT), cols(hm, (c % 2) * TT, TT), ACT.Copy).then_inc(hhi_done, 1)

                def normal(t):
                    act.wait_ge(x1_done, g0 + t + 1)
                    act.wait_ge(r_shift, g0 + t + 1)
                    for u in range(SUB):
                        ins = a.activation(cols(z, u * D, D), cols(y, u * D, D), ACT.Identity,
                                           bias=shift[:, 0, u:u + 1], scale=rstd[:, 0, u:u + 1])
                    ins.then_inc(z_done, 1)

                def turn(t):
                    if ph == 0 and is_int(t, -2):
                        wait_apart(act, kmix_ready, 1)
                    if ph == 0 and is_int(t, -1):
                        wait_apart(act, weights_ready, 1)
                    second, first, mix = is_tile(t), is_tile(t + 1), is_tile(t + 2)
                    if first:
                        hidden(t + 1, 0)
                        hidden(t + 1, 1)
                    if second:
                        masked_high(t, 2)
                    if mix:
                        middle(t + 2)
                    if second:
                        masked_high(t, 3)
                    if first:
                        hidden(t + 1, 2)
                    if is_tile(t + 4):
                        normalised(t + 4)
                    if is_tile(t - 1) and not is_int(t, NTT):
                        normal(t - 1)
                    if second:
                        masked_high(t, 4)
                    if first:
                        hidden(t + 1, 3)
                        one_hot(t + 1)
                    if is_tile(t + 4):
                        transposed(t + 4, 0)
                    if mix:
                        x_high(t + 2)
                    if first:
                        hidden(t + 1, 4)
                    if is_tile(t + 4):
                        transposed(t + 4, 1)
                    if first:
                        masked_high(t + 1, 0)
                        masked_high(t + 1, 1)
                    if is_tile(t + 4):
                        keep(t + 4)

                over_turns(act, turn)

            def attention(b):
                def key_rows(t):
                    rows = rows_in[t if isinstance(t, int) else NT - 1]
                    first = isinstance(t, int) and t < EARLY
                    if first:
                        act.wait_ge(f_scaled, b * EARLY + t + 1)
                        scales, shifts, done = key_rstd[:, t, :], key_shift[:, t, :], a_rows[t]
                    else:
                        act.wait_ge(a_shift, b * (NT - EARLY) + t - EARLY + 1)
                        scales, shifts, done = rstd[:, FIRST_SET, :], shift[:, FIRST_SET, :], a_done
                    for u in range(SUB):
                        ins = a.activation(cols(rows, u * D, D), cols(rows, u * D, D), ACT.Identity,
                                           bias=shifts[:, u:u + 1], scale=scales[:, u:u + 1])
                    ins.then_inc(done, 1)

                def key_high(t):
                    rows_wait(act, b, t)
                    a.activation(cols(KV_hi, t * SUB * D, SUB * D), rows_in[t if isinstance(t, int) else NT - 1],
                                 ACT.Copy).then_inc(a_hi, 1)

                def keyT_high(t, c, bank):
                    act.wait_ge(aT_psum, DC * (b * NT + t) + c + 1)
                    a.activation(cols(KT_hi, c * S + t * TT, TT), PS[:, bank + c, :], ACT.Copy)\
                        .then_inc(aT_hi, 1)

                def keysT_high(t):
                    for c in range(DC):
                        keyT_high(t, c, key_bank(t))

                def q_high(j, c):
                    act.wait_ge(q_psum, DC * (b * NT + j) + c + 1)
                    a.activation(cols(q_hi, (j & 1) * (DC * TT) + c * TT, TT), ps_x[:, c, :], ACT.Copy,
                                 scale=QS / (XS * WS)).then_inc(q_hi_done, 1)

                def absolute(i, diagonal, before, ring_m):
                    lo = i * P if diagonal else 0
                    act.wait_ge(s_psum, before + i + 1)
                    a.activation(cols(ring, ring_m + i * TT + lo, TT - lo), ps_s[:, i, lo:], ACT.Abs,
                                 scale=1.0 / (QS * XS * D ** 0.5)).then_inc(abs_done, 1)

                def probability(i, diagonal, before, ring_n):
                    lo = i * P if diagonal else 0
                    k = before + i
                    p = pf[:, (i % 2) * TT + lo:(i % 2 + 1) * TT]
                    act.wait_ge(plo_done, k + 1)
                    act.wait_ge(sub_done, k + 1)
                    a.activation(p, cols(ring, ring_n + i * TT + lo, TT - lo), ACT.Exp)\
                        .then_inc(exp_done, 1)
                    act.wait_ge(pv_done, k + 1)
                    act.wait_ge(exp_done, k + 1)
                    a.activation(p_hi[:, i * TT + lo:(i + 1) * TT], p, ACT.Copy).then_inc(phi_done, 1)

                def weighted(j):
                    act.wait_ge(pv_done, blocks(act, b, j + 1, 0) + SUB)
                    if has_o(j):
                        act.wait_ge(out_psum, SUB * (b * NT + j))
                    a.activation(U[:, 0:TT], ps_u[:, 0, :], ACT.Copy)
                    a.activation(U[:, TT:], ps_u[:, 1, :], ACT.Copy).then_inc(u_done, 1)

                def group(before, score, value, beside):
                    if before:
                        p_before, p_ring = blocks(act, b, *before[:2]), ring_at(act, *before[:2])
                    if score:
                        s_before, s_ring = blocks(act, b, *score[:2]), ring_at(act, *score[:2])
                    if value:
                        v_before, v_ring = blocks(act, b, *value[:2]), ring_at(act, *value[:2])
                    for i in range(SUB):
                        if value:
                            probability(i, value[2], v_before, v_ring)
                        if before and i == 0:
                            absolute(SUB - 1, before[2], p_before, p_ring)
                        if score and i >= 1:
                            absolute(i - 1, score[2], s_before, s_ring)
                        beside(i)

                def step(j):
                    more, more2 = has_next(j, 1), has_next(j, 2)

                    def maxima():
                        act.wait_ge(maxrow_psum, b * NT + j + 1)
                        a.activation(max_row[:, :], ps_x[:, 1, :], ACT.Copy, bias=-P_LOG).then_inc(spare_free[1], 1)

                    def first(i):
                        if i == 1:
                            maxima()
                        if is_int(j, 0) and i >= 2:
                            q_high(j + 2, i - 2)

                    def first_pair(i):
                        if more2 and i == 3:
                            for c in range(DC):
                                q_high(j + 2, c)
                        if has_keys(j) and i == 3:
                            key_rows(j + KEYS)

                    def last_pair(i):
                        if more2:
                            if is_int(j, 1) and i in (2, 3):
                                q_high(j + 2, i - 2)
                        if has_keys(j) and i == 0:
                            key_high(j + KEYS)
                        if has_keys(j) and i >= 2:
                            keyT_high(j + KEYS, i - 2, SPARE_BANK)

                    if has_o(j):
                        weighted(j - 1)
                    if more:
                        group((j + 1, 0, False), (j + 1, 1, is_int(j, 0)), None, first)
                    else:
                        maxima()
                    over_pairs(act, j, lambda m: group((j + 1, m + 1, False) if more else None,
                                                       (j + 1, m + 2, False) if more else None,
                                                       (j, m, False), first_pair if is_int(m, 0) else lambda i: None))
                    if has_o(j):
                        group((j + 1, j, False) if more else None, (j + 1, j + 1, True) if more else None,
                              (j, j - 1, False), last_pair)
                    group((j + 1, j + 1, True) if more else None, (j + 2, 0, False) if more2 else None,
                          (j, j, True), lambda i: None)

                key_rows(0)
                keysT_high(0)
                key_rows(1)
                keysT_high(1)
                key_rows(2)
                act.wait_ge(stored, 16 * (NTT - 2 + NT))
                for j in range(2):
                    for c in range(DC):
                        q_high(j, c)
                    keysT_high(j + 2)
                    key_high(j)
                group(None, (0, 0, True), None, lambda i: None)
                absolute(SUB - 1, True, blocks(act, b, 0, 0), ring_at(act, 0, 0))
                keysT_high(EARLY - 1)
                for t in range(2, EARLY):
                    key_high(t)
                group(None, (1, 0, False), None, lambda i: None)
                over_steps(act, step)
                weighted(NT - 1)

            ffn(0)
            with act.Fori(0, B) as b:
                attention(b)
            attention_over(act)
            ffn(1)

        @block.tensor
        def _(pe):
            t_ = nc.tensor

            def split_product(dst, pairs, start, stop, skip=False):
                last = 3 * len(pairs) - 1
                n = 0
                for (w_h, w_l), (x_h, x_l) in pairs:
                    for w, xx in ((w_h, x_h), (w_h, x_l), (w_l, x_h)):
                        ins = t_.matmul(dst, w, xx, start=start and n == 0, stop=stop and n == last,
                                        skip_group_check=skip)
                        n += 1
                return ins

            def transpose_rows(dst, rows, c):
                for u in range(SUB):
                    ins = t_.transpose(dst[:, u * P:(u + 1) * P], cols(rows, u * D + c * P, P), ident[:, :])
                return ins

            def fold():
                pe.wait_ge(attention_weights_in, 16 * ATTENTION_LOADS)
                for c in range(DC):
                    for d in range(DC):
                        ins = t_.transpose(PS[:, 6, d * D + c * P:d * D + (c + 1) * P],
                                           wo_s[:, c * D + d * P:c * D + (d + 1) * P], ident[:, :])
                ins.then_inc(woT_psum, 1)
                pe.wait_ge(folded, 3 * DC)
                wq_f, wk_f, wv_f = (wqkv_s[:, i * DC * D:(i + 1) * DC * D] for i in range(3))
                for d in range(DC):
                    for c in range(DC):
                        ins = t_.matmul(PS[:, d, 0:D], wq_f[:, c * D + d * P:c * D + (d + 1) * P],
                                        wk_f[:, c * D:(c + 1) * D], start=c == 0, stop=c == DC - 1)
                ins.then_inc(wqk_psum, 1)
                pe.wait_ge(woT_done, 1)
                for d in range(DC):
                    for c in range(DC):
                        ins = t_.matmul(PS[:, 2 + d, 0:D], wv_f[:, c * D + d * P:c * D + (d + 1) * P],
                                        wo_t[:, c * D:(c + 1) * D], start=c == 0, stop=c == DC - 1)
                ins.then_inc(wvo_psum, 1)

            pe.sem_inc(pv_done, SUB)
            pe.wait_ge(pool_const, POOL_CONSTS)

            def ffn(ph):
                g0 = ph * NTT

                def transposed(t, c):
                    k = DC * (g0 + t) + c
                    if beside(ph, t):
                        pe.wait_ge(n_beside, beside(ph, t))
                    else:
                        pe.wait_ge(n_done, g0 + t + 1)
                    pe.wait_ge(nT_done, k if early(t) and t < AHEAD - 1 and c == 1 else k + 1)
                    transpose_rows(rows_bank(t, c), normal_rows(t), c).then_inc(nT_psum, 1)

                def hidden(t, c):
                    k = HC * (g0 + t)
                    pe.wait_ge(hb_done, k + (2, 1, 3, 4, 5)[c])
                    x_at = (t & 1) * (DC * TT)
                    split_product(ps_h[:, c % 2, :],
                                  [((w1_hi[:, d, c * P:(c + 1) * P], w1_lo[:, d, c * P:(c + 1) * P]),
                                    (cols(xhi, x_at + d * TT, TT), cols(xlo, x_at + d * TT, TT)))
                                   for d in range(DC)], True, True).then_inc(h_psum, 1)

                def route(t):
                    pe.wait_ge(tanh_done, g0 + t + 1)
                    for u in range(SUB):
                        ins = t_.matmul(ps_route[:, u, :], th[:, u * P:(u + 1) * P], wo2[:, :], start=True, stop=True)
                    ins.then_inc(route_psum, 1)

                def choice(t):
                    pe.wait_ge(oh_done, g0 + t + 1)
                    for u in range(SUB):
                        ins = t_.transpose(ps_oh[0:NP, u * P:(u + 1) * P], oh[:, u, :], ident16[:, :])
                    ins.then_inc(ohT_psum, 1)

                def mask(t, c):
                    k = HC * (g0 + t)
                    if c == 0:
                        pe.wait_ge(ohT_done, g0 + t + 1)
                    pe.wait_ge(hm_done, k + (2, 2, 3, 4, 5)[c])
                    t_.matmul(ps_m[:, c % 2, :], expand[:, c, :], oh_t[:, :], start=True, stop=True)\
                        .then_inc(mask_psum, 1)

                def path(t, c):
                    if c == 0:
                        pe.wait_ge(y_done, 2 * (g0 + t) + 2)
                    pe.wait_ge(hlo_done, HC * (g0 + t) + c + 1)
                    for u in range(SUB):
                        at = c * TT + u * P
                        ins = split_product(ps_o[:, u // 2, (u % 2) * D:(u % 2 + 1) * D],
                                            [((cols(hhi, at, P), cols(hlo, at, P)), (w2_hi[:, c, :], w2_lo[:, c, :]))],
                                            c == 0 and u % 2 == 0, c == HC - 1, skip=True)
                    if c == HC - 1:
                        ins.then_inc(o_psum, 1)

                def turn(t):
                    if ph == 0 and is_int(t, -1):
                        wait_apart(pe, weights_ready, 1)
                    if ph == 0 and is_int(t, 0):
                        wait_apart(pe, weights_ready, 2)
                    second, first = is_tile(t), is_tile(t + 1)
                    if first:
                        pe.wait_ge(xlo_done, DC * (g0 + t + 1) + DC)
                        hidden(t + 1, 0)
                    if second:
                        mask(t, 2)
                    if first:
                        hidden(t + 1, 1)
                    if second:
                        path(t, 0)
                        mask(t, 3)
                    if first:
                        route(t + 1)
                        hidden(t + 1, 2)
                    if second:
                        path(t, 1)
                        mask(t, 4)
                    if first:
                        hidden(t + 1, 3)
                    if second:
                        path(t, 2)
                    if is_tile(t + 4):
                        transposed(t + 4, 0)
                    if first:
                        choice(t + 1)
                        hidden(t + 1, 4)
                    if second:
                        path(t, 3)
                    if is_tile(t + 4):
                        transposed(t + 4, 1)
                    if first:
                        mask(t + 1, 0)
                        mask(t + 1, 1)
                    if second:
                        path(t, 4)

                over_turns(pe, turn)
                if ph == 0:
                    fold()

            def attention(b):
                def keys(t, c, bank):
                    rows_wait(pe, b, t)
                    transpose_rows(PS[:, bank + c, :], rows_in[t if isinstance(t, int) else NT - 1], c)\
                        .then_inc(aT_psum, 1)

                def keys_wait(t):
                    pe.wait_ge(aT_lo, DC * (b * NT + t) + 2 * DC)

                def query(j, k, c):
                    pe.wait_ge(spare_free[c], k + 1)
                    split_product(ps_x[:, c, :],
                                  [((wqk_hi[:, d, c * P:(c + 1) * P], wqk_lo[:, d, c * P:(c + 1) * P]),
                                    (cols(KT_hi, d * S + j * TT, TT), cols(KT_lo, d * S + j * TT, TT)))
                                   for d in range(DC)], True, True).then_inc(q_psum, 1)

                def scores(before, m, i, q, diagonal):
                    lo = i * P if diagonal else 0
                    pe.wait_ge(abs_done, before + i + 1)
                    at = m * TT + i * P
                    split_product(ps_s[:, i, lo:],
                                  [((cols(KT_hi, d * S + at, P), cols(KT_lo, d * S + at, P)),
                                    (cols(q_hi, q + lo + d * TT, TT - lo), cols(q_lo, q + lo + d * TT, TT - lo)))
                                   for d in range(DC)], True, True).then_inc(s_psum, 1)

                def values(before, m, i, diagonal):
                    lo = i * P if diagonal else 0
                    pe.wait_ge(plo_done, before + i + 3)
                    at = (m * SUB + i) * D
                    for c in range(DC):
                        ins = split_product(ps_u[:, c, lo:],
                                            [((cols(KV_hi, at + c * P, P), cols(KV_lo, at + c * P, P)),
                                              (p_hi[:, i * TT + lo:(i + 1) * TT], p_lo[:, i * TT + lo:(i + 1) * TT]))],
                                            is_int(m, 0) and i == 0, i == SUB - 1, skip=True)
                    ins.then_inc(pv_done, 1)

                def output(s, k, u):
                    if u == 0:
                        pe.wait_ge(u_done, s + 2)
                    if u < 2:
                        pe.wait_ge(spare_free[u], k + 1)
                    else:
                        pe.wait_ge(x2_done, SUB * s + u - 1)
                    for c in range(DC):
                        ins = t_.matmul(ps_x[:, u % 2, 0:D + 1], U[:, c * TT + u * P:c * TT + (u + 1) * P],
                                        wvo[:, c, 0:D + 1], start=c == 0, stop=c == DC - 1)
                    ins.then_inc(out_psum, 1)

                def group(score, value, beside):
                    if score:
                        s_before, q = blocks(pe, b, *score[:2]), (score[0] & 1) * (DC * TT)
                    if value:
                        v_before = blocks(pe, b, *value[:2])
                    if score and is_int(score[1], 0):
                        uses = 0 if is_int(score[0], 0) else 2 * score[0] - 1
                        for c in range(DC):
                            pe.wait_ge(spare_free[c], b * SPARE + uses + 2)
                    for i in range(SUB):
                        if score:
                            scores(s_before, score[1], i, q, score[2])
                        if value:
                            values(v_before, value[1], i, value[2])
                        beside(i)

                def step(j):
                    s = b * NT + j
                    k = b * SPARE + spare(j)

                    if has_o(j) and not is_int(j, 1):
                        pe.wait_ge(x2_done, SUB * s - SUB - 1)
                    pe.wait_ge(spare_free[0], k + 1)
                    pe.wait_ge(max_done, blocks(pe, b, j + 1, 0))
                    for u in range(SUB):
                        ins = t_.transpose(ps_x[:, 0, u * P:(u + 1) * P], run_max[:, u * P:(u + 1) * P], ident[:, :])
                    ins.then_inc(maxT_psum, 1)

                    def max_row_back():
                        if has_o(j) and not is_int(j, 1):
                            pe.wait_ge(x2_done, SUB * s - SUB)
                        pe.wait_ge(spare_free[0], k + 2)
                        pe.wait_ge(spare_free[1], k + 1)
                        for u in range(SUB):
                            ins = t_.transpose(ps_x[:, 1, u * P:(u + 1) * P], max_col[:, u:u + 1].to_broadcast([P, P]),
                                               ident[:, :])
                        ins.then_inc(maxrow_psum, 1)

                    def first(i):
                        if i == 0:
                            max_row_back()
                        if is_int(j, 0) and i >= 2:
                            query(j + 2, k + 1, i - 2)

                    def first_pair(i):
                        if has_next(j, 2) and i < DC:
                            if i == 0:
                                keys_wait(j + 2)
                            query(j + 2, k + 1, i)
                        if is_int(j, NT - 1):
                            for u in ((2,), (3,), (), ())[i]:
                                output(s - 1, k + 1, u)

                    def last_pair(i):
                        if is_int(j, 1):
                            first_pair(i)
                        if has_keys(j) and i < DC:
                            pe.wait_ge(spare_free[i], k + 2 + int(has_next(j, 2)))
                            keys(j + KEYS, i, SPARE_BANK)
                        if i == SUB - 1 and not is_int(j, NT - 1):
                            if has_keys(j):
                                pe.wait_ge(aT_lo, DC * (b * NT + j + KEYS) + DC + 1)
                            output(s - 1, k + 1 + int(has_next(j, 2)), 0)

                    def diagonal(i):
                        if has_o(j) and i < SUB - 1 and not is_int(j, NT - 1):
                            if has_keys(j) and i == 0:
                                keys_wait(j + KEYS)
                            output(s - 1, k + 1 + int(has_next(j, 2)), i + 1)

                    if has_next(j, 1):
                        group((j + 1, 1, is_int(j, 0)), None, first)
                    else:
                        max_row_back()
                    if is_int(j, 0):
                        keys_wait(EARLY - 1)
                        pe.wait_ge(a_lo, b * NT + EARLY)
                    elif isinstance(j, int) and j >= EARLY:
                        pe.wait_ge(a_lo, b * NT + j + 1)
                    wait_apart(pe, u_done, s + 1)

                    if is_int(j, NT - 1):
                        for u in range(2):
                            output(s - 1, k + 1, u)
                    over_pairs(pe, j, lambda m: group((j + 1, m + 2, False) if has_next(j, 1) else None, (j, m, False),
                                                      first_pair if is_int(m, 0) else lambda i: None))
                    if has_o(j):
                        group((j + 1, j + 1, True) if has_next(j, 1) else None, (j, j - 1, False), last_pair)
                    group((j + 2, 0, False) if has_next(j, 2) else None, (j, j, True), diagonal)

                pe.wait_ge(y_done, 2 * NTT + 2)
                pe.wait_ge(u_done, b * NT + 1)
                for t in range(EARLY - 1):
                    if t == 1:
                        pe.wait_ge(fold_step, FOLD_STEPS)
                        pe.wait_ge(abs_done, b * BLOCKS + SUB)
                        pe.wait_ge(x2_stored, 16 * (b * NT) + 1)
                    if t >= 2:
                        keys_wait(t - 2)
                    for c in range(DC):
                        keys(t, c, key_bank(t))
                    if t in (1, 2):
                        keys_wait(t - 1)
                        for c in range(DC):
                            query(t - 1, b * SPARE + t - 1, c)
                keys_wait(EARLY - 2)
                group((0, 0, True), None, lambda i: None)
                for c in range(DC):
                    keys(EARLY - 1, c, key_bank(EARLY - 1))
                group((1, 0, False), None, lambda i: None)
                over_steps(pe, step)
                pe.wait_ge(x2_done, SUB * (b * NT + NT - 1))
                for u in range(SUB):
                    output(b * NT + NT - 1, b * SPARE + SPARE, u)

            ffn(0)
            with pe.Fori(0, B) as b:
                attention(b)
            attention_over(pe)
            ffn(1)


_INS = ["L0_attn_x", "L0_attn_Wq", "L0_attn_bq", "L0_attn_Wk", "L0_attn_bk", "L0_attn_Wv", "L0_attn_bv", "L0_attn_Wo",
        "L0_attn_bo", "L0_ffn_mix_kernel", "L0_ffn_W1", "L0_ffn_b1", "L0_ffn_W2", "L0_ffn_b2", "L0_ffn_Wo1",
        "L0_ffn_bo1", "L0_ffn_Wo2", "L0_ffn_bo2", "L0_ffn_gamma", "L0_ffn_beta"]


def kernel(**inputs):
    import numpy as _np
    import concourse.bacc as _bacc
    from concourse.bass_utils import run_bass_kernel_spmd as _run

    nc = _bacc.Bacc("TRN2", target_bir_lowering=False, num_devices=1)
    arrays, args = {}, []
    for name in _INS:
        a = _np.ascontiguousarray(inputs[name])
        arrays[f"in_{name}"] = a
        args.append(nc.dram_tensor(f"in_{name}", a.shape, mybir.dt.from_np(a.dtype), kind="ExternalInput").ap())
    out = nc.dram_tensor("out_0", (B, S, D), F32, kind="ExternalOutput").ap()
    macaron(nc, *args, out)
    r = _run(nc, [arrays], core_ids=[0])
    return r.results[0]["out_0"]
```
